# Optimizing a Trainium2 kernel written in Bass

```python
import numpy as np
import jax
import jax.numpy as jnp

def _softmax(x, axis=-1):
    return jax.nn.softmax(x, axis=axis)

def _gelu(x):
    return jax.nn.gelu(x, approximate=True)

def _silu(x):
    return jax.nn.silu(x)

def _sigmoid(x):
    return jax.nn.sigmoid(x)

def _layernorm(x, axis=-1, eps=1e-05):
    m = jnp.mean(x, axis=axis, keepdims=True)
    v = jnp.var(x, axis=axis, keepdims=True)
    return (x - m) / jnp.sqrt(v + eps)

def _scatter_add(tgt, idx, src, axis=0):
    return tgt.at[idx].add(src)

def _segment_sum(src, seg, n):
    return jax.ops.segment_sum(src, seg, n)
kernel_name = 'mk_recurrent_d1_jaxref_r2_4894c2'

def setup_inputs(seed: int=0):
    np.random.seed(seed)
    _w = jnp.asarray

    def _L0_attn_setup():
        import jax, jax.numpy as jnp
        import numpy as np
        LN_EPS = 1e-05
        key = jax.random.key(seed)
        ks = jax.random.split(key, 5)
        B, S, E, H = (4, 512, 512, 16)
        sd = E ** (-0.5)
        return {'x': jax.random.normal(ks[0], (B, S, E), jnp.float32), 'Wq': jax.random.normal(ks[1], (E, E), jnp.float32) * sd, 'Wk': jax.random.normal(ks[2], (E, E), jnp.float32) * sd, 'Wv': jax.random.normal(ks[3], (E, E), jnp.float32) * sd, 'bias_table': jax.random.normal(ks[4], (2 * S - 1, H), jnp.float32) * 0.02, 'ln_gamma': jnp.ones((E,), jnp.float32), 'ln_beta': jnp.zeros((E,), jnp.float32)}
    _L0_attn_in = _L0_attn_setup()

    def _L0_ffn_setup():
        import jax, jax.numpy as jnp
        import numpy as np
        import math
        BETA = 0.9
        THRESHOLD = 1.0
        NUM_STEPS = 5
        ALPHA = 2.0

        @jax.custom_vjp
        def spike_fn(u):
            return (u > 0).astype(u.dtype)

        def _spike_fwd(u):
            return (spike_fn(u), u)

        def _spike_bwd(u, g):
            s = jnp.pi / 2.0 * ALPHA * u
            return (g * (ALPHA / 2.0) / (1.0 + s * s),)
        spike_fn.defvjp(_spike_fwd, _spike_bwd)
        key = jax.random.key(seed)
        k1, k2, k3 = jax.random.split(key, 3)
        n_embd = 512
        x = jax.random.normal(k1, (4, 1024, n_embd), dtype=jnp.float32)
        W_fc = jax.random.normal(k2, (4 * n_embd, n_embd), dtype=jnp.float32) / math.sqrt(n_embd)
        W_proj = jax.random.normal(k3, (n_embd, 4 * n_embd), dtype=jnp.float32) / math.sqrt(4 * n_embd)
        return {'x': x, 'W_fc': W_fc, 'W_proj': W_proj}
    _L0_ffn_in = _L0_ffn_setup()
    _d = {'L0_attn_x': _L0_attn_in['x'], 'L0_attn_Wq': _L0_attn_in['Wq'], 'L0_attn_Wk': _L0_attn_in['Wk'], 'L0_attn_Wv': _L0_attn_in['Wv'], 'L0_attn_bias_table': _L0_attn_in['bias_table'], 'L0_attn_ln_gamma': _L0_attn_in['ln_gamma'], 'L0_attn_ln_beta': _L0_attn_in['ln_beta'], 'L0_ffn_W_fc': _L0_ffn_in['W_fc'], 'L0_ffn_W_proj': _L0_ffn_in['W_proj']}
    _x0 = _d['L0_attn_x']
    _d['L0_attn_x'] = jax.random.normal(jax.random.fold_in(jax.random.key(seed), 1), (8, 1024, 512), dtype=_x0.dtype)
    del _x0
    return _d

def reference(L0_attn_x, L0_attn_Wq, L0_attn_Wk, L0_attn_Wv, L0_attn_bias_table, L0_attn_ln_gamma, L0_attn_ln_beta, L0_ffn_W_fc, L0_ffn_W_proj):

    def _L0_attn_ref(x, Wq, Wk, Wv, bias_table, ln_gamma, ln_beta):
        import jax, jax.numpy as jnp
        import numpy as np
        LN_EPS = 1e-05
        B, S, E = x.shape
        H = bias_table.shape[1]
        d = E // H
        scale = E ** (-0.5)
        q = (x @ Wq.T).reshape(B, S, H, d).transpose(0, 2, 1, 3)
        k = (x @ Wk.T).reshape(B, S, H, d).transpose(0, 2, 1, 3)
        v = (x @ Wv.T).reshape(B, S, H, d).transpose(0, 2, 1, 3)
        attn = jax.nn.softmax(jnp.einsum('bhsd,bhtd->bhst', q, k) * scale, axis=-1)
        rel_idx = jnp.arange(S)[:, None] - jnp.arange(S)[None, :] + (S - 1)
        rel_bias = bias_table[rel_idx].transpose(2, 0, 1)
        attn = attn + rel_bias[None]
        out = jnp.einsum('bhst,bhtd->bhsd', attn, v)
        out = out.transpose(0, 2, 1, 3).reshape(B, S, E)
        mu = out.mean(-1, keepdims=True)
        var = out.var(-1, keepdims=True)
        out = (out - mu) * jax.lax.rsqrt(var + LN_EPS) * ln_gamma + ln_beta
        return out

    def _L0_ffn_ref(x, W_fc, W_proj):
        import jax, jax.numpy as jnp
        import numpy as np
        import math
        BETA = 0.9
        THRESHOLD = 1.0
        NUM_STEPS = 5
        ALPHA = 2.0

        @jax.custom_vjp
        def spike_fn(u):
            return (u > 0).astype(u.dtype)

        def _spike_fwd(u):
            return (spike_fn(u), u)

        def _spike_bwd(u, g):
            s = jnp.pi / 2.0 * ALPHA * u
            return (g * (ALPHA / 2.0) / (1.0 + s * s),)
        spike_fn.defvjp(_spike_fwd, _spike_bwd)
        h = jnp.square(jax.nn.relu(jnp.einsum('bsd,fd->bsf', x, W_fc)))
        y = jnp.einsum('bsf,df->bsd', h, W_proj)

        def step(mem, _):
            reset = jax.lax.stop_gradient(spike_fn(mem - THRESHOLD))
            mem_new = BETA * mem + y - reset * THRESHOLD
            spk = spike_fn(mem_new - THRESHOLD)
            return (mem_new, spk)
        mem0 = jnp.zeros_like(y)
        _, spks = jax.lax.scan(step, mem0, None, length=NUM_STEPS)
        return jnp.sum(spks, axis=0) / NUM_STEPS
    x = L0_attn_x
    xn = _layernorm(x, axis=-1)
    s = _L0_attn_ref(xn, L0_attn_Wq, L0_attn_Wk, L0_attn_Wv, L0_attn_bias_table, L0_attn_ln_gamma, L0_attn_ln_beta)
    g = _silu(_L0_ffn_ref(xn, L0_ffn_W_fc, L0_ffn_W_proj))
    x = x + s * g
    return x

_drawn_inputs = setup_inputs


def setup_inputs(seed=0):
    import zlib

    import numpy as np

    out = dict(_drawn_inputs(seed))
    spreads = {'L0_attn_ln_gamma': (1.0, 0.2), 'L0_attn_ln_beta': (0.0, 0.1)}
    factors = {'L0_attn_Wq': 6.036, 'L0_attn_Wk': 5.863}
    for name, (base, spread) in spreads.items():
        noise = np.random.default_rng([zlib.crc32(name.encode()), seed]).standard_normal(out[name].shape)
        drawn = base * np.exp(spread * noise) if base else spread * noise
        out[name] = jnp.asarray(drawn.astype(out[name].dtype))
    for name, factor in factors.items():
        out[name] = (out[name] * factor).astype(out[name].dtype)
    return out
```

```python
from contextlib import ExitStack

import concourse.bass as bass
from concourse import mybir

ALU = mybir.AluOpType
ACT = mybir.ActivationFunctionType
F32 = mybir.dt.float32
F16 = mybir.dt.float16
BF16 = mybir.dt.bfloat16
I32 = mybir.dt.int32
AX = mybir.AxisListType.X
P = 128
BANK = 512
LN_EPS = 1e-5
STEPS = 5
BETA = 0.9
EXPONENT = 0x7F800000
EXP_LN_SET = 6
EB = 4
FB = 16
TERMS = ((0, 0), (0, 1), (1, 0))


def load_exp_ln_tables(nc, act):
    act.add_instruction(mybir.InstLoadActFuncSet(
        name=nc.get_next_instruction_name(), engine=mybir.EngineType.Activation,
        ins=[], outs=[], act_func_set_id=EXP_LN_SET))


def prepare_weights(nc, d, w):
    with ExitStack() as ctx:
        sb = lambda name, shape, dt: ctx.enter_context(nc.sbuf_tensor(name, shape, dt))
        sem = lambda name: ctx.enter_context(nc.semaphore(name))
        stage_fc = sb("stage_fc", [P, EB, 2048], F32)
        stage_pr = sb("stage_pr", [P, FB, 512], F32)
        stage_qkv = sb("stage_qkv", [P, 3, EB, 512], F32)
        square = sb("square", [P, 2, 2048], BF16)
        ones = sb("ones", [P, P], BF16)
        norms = sb("norms", [P, 8], F32)
        work = sb("work", [P, 24], F32)
        rows, known = d["tableT"].shape
        table = sb("table", [rows, d["table_ext"].shape[1]], F32)
        ps = ctx.enter_context(nc.psum_tensor("ps_norm", [P, 8, BANK], F32))

        loaded = sem("loaded")
        ones_set = sem("ones_set")
        ident_step = sem("ident_step")
        squared = sem("squared")
        summed = sem("summed")
        normed = sem("normed")
        logged = sem("logged")
        rooted = sem("rooted")
        small = sem("small")
        scaled = sem("scaled")
        hi_done = sem("hi_done")
        lo_done = sem("lo_done")
        table_loaded = sem("table_loaded")
        table_grown = sem("table_grown")
        block = ctx.enter_context(nc.Block())

        fc = [stage_fc[:, k, :] for k in range(EB)]
        pr = [stage_pr[:, 4 * k:4 * k + 4, :].rearrange("p a n -> p (a n)") for k in range(4)]
        qkv = [stage_qkv[:, m, :, :].rearrange("p a n -> p (a n)") for m in range(3)]
        pieces = fc + pr + qkv
        SCALE_FC, SCALE_PR, SCALE_Q, SCALE_K, SCALE_V = 12, 13, 14, 15, 16
        scale_of = [SCALE_FC] * 4 + [SCALE_PR] * 4 + [SCALE_Q, SCALE_K, SCALE_V]
        hi_of = ([w["fc"][:, 0, k, :] for k in range(EB)]
                 + [w["pr"][:, 0, 4 * k:4 * k + 4, :].rearrange("p a n -> p (a n)") for k in range(4)]
                 + [w[m][:, 0, :, :].rearrange("p a n -> p (a n)") for m in "qkv"])
        lo_of = ([w["fc"][:, 1, k, :] for k in range(EB)]
                 + [w["pr"][:, 1, 4 * k:4 * k + 4, :].rearrange("p a n -> p (a n)") for k in range(4)]
                 + [w[m][:, 1, :, :].rearrange("p a n -> p (a n)") for m in "qkv"])

        @block.sync
        def _(sp):
            sp.dma_start(table[:, :known], d["tableT"]).then_inc(table_loaded, 16)
            for k in range(EB):
                sp.dma_start(stage_fc[:, k, :], d["fcT"].rearrange("(k p) n -> k p n", p=P)[k]).then_inc(loaded, 16)
            sp.dma_start(stage_qkv[:, 0], d["qT"].rearrange("(k p) n -> p k n", p=P)).then_inc(loaded, 16)
            sp.dma_start(stage_qkv[:, 1], d["kT"].rearrange("(k p) n -> p k n", p=P)).then_inc(loaded, 16)
            sp.dma_start(stage_qkv[:, 2], d["vT"].rearrange("(k p) n -> p k n", p=P)).then_inc(loaded, 16)
            for k in range(4):
                sp.dma_start(stage_pr[:, 4 * k:4 * k + 4], d["prT"].rearrange("(k p) n -> p k n", p=P)[:, 4 * k:4 * k + 4]).then_inc(loaded, 16)
            sp.wait_ge(table_grown, 1)
            sp.dma_start(d["table_ext"], table[:]).then_inc(table_loaded, 16)
            sp.wait_ge(loaded, 16 * 11)
            sp.wait_ge(table_loaded, 32)

        @block.gpsimd
        def _(pool):
            nc.gpsimd.memset(w["ident"][:], 0.0).then_inc(ident_step, 1)
            pool.wait_ge(ident_step, 1)
            nc.gpsimd.affine_select(out=w["ident"][:], in_=w["ident"][:], compare_op=ALU.not_equal, fill=1.0,
                                    base=0, pattern=[[-1, P]], channel_multiplier=1).then_inc(ident_step, 1)
            pool.wait_ge(ident_step, 2)

        @block.scalar
        def _(act):
            load_exp_ln_tables(nc, act)
            act.wait_ge(loaded, 16 * 11)
            for n, piece in enumerate(pieces):
                if n >= 2:
                    act.wait_ge(summed, n - 1)
                nc.scalar.activation(square[:, n % 2, :], piece, ACT.Square).then_inc(squared, 1)
            act.wait_ge(small, 2)
            nc.scalar.activation(work[:, 0:4], norms[:, 0:4], ACT.Ln).then_inc(logged, 1)
            act.wait_ge(logged, 1)
            nc.scalar.activation(work[:, 4:7], work[:, 0:3], ACT.Exp, scale=0.5).then_inc(rooted, 1)
            nc.scalar.activation(work[:, 7:8], work[:, 3:4], ACT.Exp, scale=0.25).then_inc(rooted, 1)
            for n, piece in enumerate(pieces):
                act.wait_ge(scaled, n + 1)
                nc.scalar.activation(hi_of[n], piece, ACT.Copy).then_inc(hi_done, 1)

        @block.tensor
        def _(pe):
            pe.wait_ge(ones_set, 1)
            for n in range(11):
                pe.wait_ge(squared, n + 1)
                for c in range(4):
                    q = square[:, n % 2, c * BANK:(c + 1) * BANK]
                    if n < 4:
                        last = nc.tensor.matmul(ps[:, c, :], ones[:], q, start=(n == 0), stop=(n == 3))
                    elif n < 8:
                        last = nc.tensor.matmul(ps[:, 4, :], ones[:], q, start=(n == 4 and c == 0), stop=(n == 7 and c == 3))
                    else:
                        last = nc.tensor.matmul(ps[:, n - 3, :], ones[:], q, start=(c == 0), stop=(c == 3))
                last.then_inc(summed, 1)

        @block.vector
        def _(dve):
            nc.vector.memset(ones[:], 1.0).then_inc(ones_set, 1)
            dve.wait_ge(table_loaded, 16)
            nc.vector.tensor_copy(table[:, known:], table[:, known - 1:known].broadcast_to([rows, table.shape[1] - known])
                                  ).then_inc(table_grown, 1)
            dve.wait_ge(summed, 4)
            nc.vector.tensor_reduce(norms[:, 0:1], ps[:, 0:4, :], mybir.AxisListType.XY, ALU.max).then_inc(normed, 1)
            dve.wait_ge(summed, 8)
            nc.vector.tensor_reduce(norms[:, 1:2], ps[:, 4, :], AX, ALU.max).then_inc(normed, 1)
            dve.wait_ge(summed, 11)
            nc.vector.tensor_reduce(norms[:, 2:3], ps[:, 7, :], AX, ALU.max).then_inc(normed, 1)
            nc.vector.tensor_reduce(norms[:, 4:5], ps[:, 5, :], AX, ALU.max).then_inc(normed, 1)
            nc.vector.tensor_reduce(norms[:, 5:6], ps[:, 6, :], AX, ALU.max).then_inc(normed, 1)
            dve.wait_ge(normed, 5)
            nc.vector.tensor_scalar(norms[:, 0:3], norms[:, 0:3], 1e-18, None, ALU.max).then_inc(normed, 1)
            nc.vector.tensor_scalar(norms[:, 4:6], norms[:, 4:6], 1e-18, None, ALU.max).then_inc(normed, 1)
            dve.wait_ge(normed, 7)
            nc.vector.reciprocal(norms[:, 6:7], norms[:, 4:5]).then_inc(small, 1)
            dve.wait_ge(small, 1)
            nc.vector.tensor_tensor(norms[:, 3:4], norms[:, 5:6], norms[:, 6:7], ALU.mult).then_inc(small, 1)
            dve.wait_ge(rooted, 2)
            nc.vector.tensor_scalar(work[:, 8:12].bitcast(I32), work[:, 4:8].bitcast(I32), EXPONENT, None,
                                    ALU.bitwise_and).then_inc(small, 1)
            dve.wait_ge(small, 3)
            nc.vector.reciprocal(work[:, 17:21], work[:, 8:12]).then_inc(small, 1)
            nc.vector.tensor_tensor(work[:, 21:22], work[:, 8:9], work[:, 8:9], ALU.mult).then_inc(small, 1)
            nc.vector.tensor_copy(work[:, SCALE_Q:SCALE_Q + 1], work[:, 11:12]).then_inc(small, 1)
            nc.vector.tensor_copy(w["unscale"][:, 1:2], work[:, 10:11]).then_inc(small, 1)
            dve.wait_ge(small, 7)
            nc.vector.tensor_scalar(work[:, SCALE_FC:SCALE_FC + 1], work[:, 17:18], 4.0, None, ALU.mult).then_inc(small, 1)
            nc.vector.tensor_scalar(work[:, SCALE_PR:SCALE_PR + 1], work[:, 18:19], 256.0, None, ALU.mult).then_inc(small, 1)
            nc.vector.tensor_copy(work[:, SCALE_V:SCALE_V + 1], work[:, 19:20]).then_inc(small, 1)
            nc.vector.tensor_copy(work[:, SCALE_K:SCALE_K + 1], work[:, 20:21]).then_inc(small, 1)
            nc.vector.scalar_tensor_tensor(w["unscale"][:, 0:1], work[:, 21:22], 1.0 / (16.0 * 256.0), work[:, 9:10],
                                           ALU.mult, ALU.mult).then_inc(small, 1)
            dve.wait_ge(small, 12)
            for n, piece in enumerate(pieces):
                dve.wait_ge(squared, n + 1)
                c = scale_of[n]
                nc.vector.tensor_scalar(piece, piece, work[:, c:c + 1], None, ALU.mult).then_inc(scaled, 1)
                if n:
                    dve.wait_ge(hi_done, n)
                    nc.vector.tensor_tensor(lo_of[n - 1], pieces[n - 1], hi_of[n - 1], ALU.subtract).then_inc(lo_done, 1)
            dve.wait_ge(hi_done, 11)
            nc.vector.tensor_tensor(lo_of[10], pieces[10], hi_of[10], ALU.subtract).then_inc(lo_done, 1)


def feed_forward(nc, d, w, NC):
    LAG = 2
    with ExitStack() as ctx:
        sb = lambda name, shape, dt: ctx.enter_context(nc.sbuf_tensor(name, shape, dt))
        pt = lambda name, shape, dt: ctx.enter_context(nc.psum_tensor(name, shape, dt))
        sem = lambda name: ctx.enter_context(nc.semaphore(name))
        ident = w["ident"]
        x_in = sb("x_in", [P, 4, 512], F32)
        xn = sb("xn", [P, 4, 512], F32)
        xnT = sb("xnT_part", [P, 2, 2, EB, 512], F16)
        stats = sb("stats", [P, 4, 6], F32)
        mv = sb("mv", [P, 4, 2], F32)
        rs = sb("rs", [P, 8, 4], F32)
        relu = sb("relu", [P, 2, 512], F32)
        hid = sb("hid", [P, 2, 512], F32)
        hid_part = sb("hid_part", [P, 4, 2, 512], F16)
        y = sb("y", [P, 4, 512], F32)
        neg_mem = sb("neg_mem", [P, 4, 512], F32)
        leak = sb("leak", [P, 4, 512], F32)
        spikes = sb("spikes", [P, 4, 512], F32)
        gate = sb("gate_out", [P, 4, 512], F32)
        ps_y = pt("ps_y", [P, 4, BANK], F32)
        ps_fc = pt("ps_fc", [P, 2, BANK], F32)
        ps_t = pt("ps_t", [P, 2, BANK], F32)

        x_loaded = sem("x_loaded")
        rows_stored = sem("rows_stored")
        stat_ready = sem("stat_ready")
        var_logged = sem("var_logged")
        rstd_guess = sem("rstd_guess")
        newton = sem("newton")
        xn_ready = sem("xn_ready")
        xt_ps = sem("xt_ps")
        xt_hi = sem("xt_hi")
        xt_lo = sem("xt_lo")
        xt_stored = sem("xt_stored")
        fc_done = sem("fc_done")
        relu_done = sem("relu_done")
        sq_done = sem("sq_done")
        hi_done = sem("hhi_done")
        lo_done = sem("hlo_done")
        proj_done = sem("proj_done")
        y_ps = sem("y_ps")
        y_ready = sem("y_ready")
        lif = sem("lif")
        sig_done = sem("sig_done")
        gate_stored = sem("gate_stored")
        block = ctx.enter_context(nc.Block())
        NL = 14

        def wait(eng, s, value):
            if not (isinstance(value, int) and value <= 0):
                eng.wait_ge(s, value)

        def chunks(eng, body, last):
            body(0, 0)
            body(1, 1)
            pairs = (last - 1) // 2
            with eng.Fori(1, pairs + 1) as i:
                body(i * 2, 0)
                body(i * 2 + 1, 1)
            for c in range(2 * pairs + 2, last + 1):
                body(c, c % 2)

        @block.sync
        def _(sp):
            def load_x(c):
                wait(sp, xn_ready, c * 4)
                sp.dma_start(x_in[:], d["x"].rearrange("(c t p) e -> c p t e", p=P, t=4)[c]).then_inc(x_loaded, 16)

            def chunk(c, par, ahead=True):
                sp.wait_ge(xt_hi, c * 4 + 4)
                sp.wait_ge(xt_lo, c * 4 + 4)
                for part in range(2):
                    sp.dma_start(d["xnT"][:, part].rearrange("c (k p) s -> c p k s", p=P)[c],
                                 xnT[:, par, part]).then_inc(xt_stored, 16)
                if isinstance(c, int) and c == 0:
                    sp.dma_start(d["table_rows"], d["table_ext"].unsqueeze(1).broadcast_to(d["table_rows"].shape)
                                 ).then_inc(rows_stored, 16)
                if ahead:
                    load_x(c + 1)
                if not (isinstance(c, int) and c < 2):
                    store_gate(c - 2)

            def store_gate(c):
                sp.wait_ge(lif, c * NL + NL)
                sp.dma_start(d["gate"].rearrange("(c t p) e -> c p t e", p=P, t=4)[c], gate[:]).then_inc(gate_stored, 16)

            load_x(0)
            chunks(sp, chunk, NC - 2)
            chunk(NC - 1, (NC - 1) % 2, ahead=False)
            store_gate(NC - 2)
            store_gate(NC - 1)
            sp.wait_ge(xt_stored, 32 * NC)
            sp.wait_ge(gate_stored, 16 * NC)
            sp.wait_ge(rows_stored, 16)

        @block.tensor
        def _(pe):
            def transpose(c, k):
                if k == 0:
                    pe.wait_ge(xn_ready, c * 4 + 4)
                n = c * 4 + k
                wait(pe, xt_hi, n - 1)
                wait(pe, xt_lo, n - 1)
                for t in range(4):
                    last = nc.tensor.transpose(ps_t[:, k % 2, t * P:(t + 1) * P], xn[:, t, k * P:(k + 1) * P], ident[:])
                last.then_inc(xt_ps, 1)

            def fc(c, par, f):
                n = c * FB + f
                if f == 0:
                    pe.wait_ge(xt_lo, c * 4 + 4)
                    pe.wait_ge(xt_hi, c * 4 + 4)
                wait(pe, relu_done, n - 1)
                m = 0
                for k in range(EB):
                    for a, b in TERMS:
                        last = nc.tensor.matmul(ps_fc[:, f % 2, :], w["fc"][:, a, k, f * P:(f + 1) * P],
                                                xnT[:, par, b, k, :], start=(m == 0), stop=(m == 11))
                        m += 1
                last.then_inc(fc_done, 1)

            def proj(c, f):
                n = c * FB + f
                pe.wait_ge(lo_done, n + 1)
                pe.wait_ge(hi_done, n + 1)
                for t in range(4):
                    if f == 0:
                        wait(pe, y_ready, (c - 1) * 4 + t + 1)
                    for m, (a, b) in enumerate(TERMS):
                        last = nc.tensor.matmul(ps_y[:, t, :], hid_part[:, f % 4, a, t * P:(t + 1) * P],
                                                w["pr"][:, b, f, :], start=(f == 0 and m == 0), stop=(f == FB - 1 and m == 2))
                    if f == FB - 1:
                        last.then_inc(y_ps, 1)
                    elif t == 3:
                        last.then_inc(proj_done, 1)

            def chunk(c, par, ahead=True):
                for f in range(FB):
                    fc(c, par, f)
                    if f >= LAG:
                        proj(c, f - LAG)
                    elif not (isinstance(c, int) and c == 0):
                        proj(c - 1, FB + f - LAG)
                    if ahead and f in (6, 8, 10, 12):
                        transpose(c + 1, (f - 6) // 2)

            for k in range(EB):
                transpose(0, k)
            chunks(pe, chunk, NC - 2)
            chunk(NC - 1, (NC - 1) % 2, ahead=False)
            for f in range(FB - LAG, FB):
                proj(NC - 1, f)

        def hidden_free(eng, c, f):
            if f >= 4:
                wait(eng, proj_done, c * (FB - 1) + f - 3)
            elif f < 3:
                wait(eng, proj_done, (c - 1) * (FB - 1) + f + FB - 3)
            else:
                wait(eng, y_ps, c * 4)

        @block.scalar
        def _(act):
            def root(c):
                act.wait_ge(stat_ready, c * 9 + 9)
                nc.scalar.activation(rs[:, 1, :], rs[:, 0, :], ACT.Ln).then_inc(var_logged, 1)
                act.wait_ge(var_logged, c + 1)
                nc.scalar.activation(rs[:, 2, :], rs[:, 1, :], ACT.Exp, scale=-0.5).then_inc(rstd_guess, 1)

            def part_hi(c, par, k):
                act.wait_ge(xt_ps, c * 4 + k + 1)
                if k == 0:
                    wait(act, xt_stored, (c - 1) * 32)
                nc.scalar.activation(xnT[:, par, 0, k, :], ps_t[:, k % 2, :], ACT.Copy).then_inc(xt_hi, 1)

            def hid_hi(c, f):
                n = c * FB + f
                act.wait_ge(sq_done, n + 1)
                hidden_free(act, c, f)
                nc.scalar.activation(hid_part[:, f % 4, 0, :], hid[:, f % 2, :], ACT.Copy).then_inc(hi_done, 1)

            def chunk(c, par, ahead=True):
                first = isinstance(c, int) and c == 0
                for f in range(FB):
                    n = c * FB + f
                    if f:
                        hid_hi(c, f - 1)
                    elif not first:
                        hid_hi(c - 1, FB - 1)
                    if f == 2 and not first:
                        copy_y(c - 1)
                    act.wait_ge(fc_done, n + 1)
                    wait(act, sq_done, n - 1)
                    nc.scalar.activation(relu[:, f % 2, :], ps_fc[:, f % 2, :], ACT.Relu).then_inc(relu_done, 1)
                    if f < 3 and not (isinstance(c, int) and c < 2):
                        sigmoid(c - 2, f)
                    if ahead and f == 2:
                        root(c + 1)
                    if ahead and f in (7, 9, 11, 13):
                        part_hi(c + 1, 1 - par, (f - 7) // 2)

            def copy_y(c):
                wait(act, lif, (c - 1) * NL + 11)
                for t in range(4):
                    act.wait_ge(y_ps, c * 4 + t + 1)
                    nc.scalar.activation(y[:, t, :], ps_y[:, t, :], ACT.Copy, scale=w["unscale"][:, 0:1]).then_inc(y_ready, 1)

            def sigmoid(c, i):
                if i == 0:
                    act.wait_ge(lif, c * NL + 13)
                    op = nc.scalar.activation(leak[:], spikes[:], ACT.Exp, scale=-1.0 / STEPS)
                else:
                    act.wait_ge(sig_done, c * 3 + i)
                    if i == 1:
                        op = nc.scalar.activation(leak[:], leak[:], ACT.Ln, bias=1.0)
                    else:
                        op = nc.scalar.activation(leak[:], leak[:], ACT.Exp, scale=-1.0)
                op.then_inc(sig_done, 1)

            load_exp_ln_tables(nc, act)
            root(0)
            for k in range(EB):
                part_hi(0, 0, k)
            chunks(act, chunk, NC - 2)
            chunk(NC - 1, (NC - 1) % 2, ahead=False)
            hid_hi(NC - 1, FB - 1)
            copy_y(NC - 1)
            for i in range(3):
                sigmoid(NC - 2, i)
            for i in range(3):
                sigmoid(NC - 1, i)

        @block.vector
        def _(dve):
            def statistics(c):
                dve.wait_ge(x_loaded, c * 16 + 16)
                for t in range(4):
                    wait(dve, stat_ready, (c - 1) * 9 + t + 5)
                    nc.vector.bn_stats(stats[:, t, :], x_in[:, t, :]).then_inc(stat_ready, 1)
                wait(dve, xn_ready, c * 4)
                dve.wait_ge(stat_ready, c * 9 + 4)
                nc.vector.memset(rs[:, 7, :], 0.0)
                for t in range(4):
                    nc.vector.bn_aggr(mv[:, t, :], stats[:, t, :]).then_inc(stat_ready, 1)
                dve.wait_ge(stat_ready, c * 9 + 8)
                wait(dve, newton, c * 4)
                nc.vector.tensor_scalar(rs[:, 0, :], mv[:, :, 1], LN_EPS, None, ALU.add).then_inc(stat_ready, 1)

            def normalise(c):
                dve.wait_ge(rstd_guess, c + 1)
                nc.vector.tensor_tensor(rs[:, 3, :], rs[:, 2, :], rs[:, 2, :], ALU.mult).then_inc(newton, 1)
                dve.wait_ge(newton, c * 4 + 1)
                nc.vector.tensor_tensor(rs[:, 4, :], rs[:, 3, :], rs[:, 0, :], ALU.mult).then_inc(newton, 1)
                dve.wait_ge(newton, c * 4 + 2)
                nc.vector.tensor_scalar(rs[:, 5, :], rs[:, 4, :], -0.5, 1.5, ALU.mult, ALU.add).then_inc(newton, 1)
                dve.wait_ge(newton, c * 4 + 3)
                nc.vector.tensor_tensor(rs[:, 6, :], rs[:, 5, :], rs[:, 2, :], ALU.mult).then_inc(newton, 1)
                dve.wait_ge(newton, c * 4 + 4)
                wait(dve, xt_ps, c * 4)
                for t in range(4):
                    nc.vector.tensor_scalar(xn[:, t, :], x_in[:, t, :], mv[:, t, 0:1], rs[:, 6, t:t + 1],
                                            ALU.subtract, ALU.mult).then_inc(xn_ready, 1)

            def part_lo(c, par, k):
                dve.wait_ge(xt_hi, c * 4 + k + 1)
                nc.vector.tensor_tensor(xnT[:, par, 1, k, :], ps_t[:, k % 2, :], xnT[:, par, 0, k, :],
                                        ALU.subtract).then_inc(xt_lo, 1)

            def square(c, f):
                n = c * FB + f
                dve.wait_ge(relu_done, n + 1)
                wait(dve, hi_done, n - 1)
                wait(dve, lo_done, n - 1)
                nc.vector.tensor_tensor(hid[:, f % 2, :], relu[:, f % 2, :], relu[:, f % 2, :], ALU.mult).then_inc(sq_done, 1)

            def hid_lo(c, f):
                n = c * FB + f
                dve.wait_ge(hi_done, n + 1)
                nc.vector.tensor_tensor(hid_part[:, f % 4, 1, :], hid[:, f % 2, :], hid_part[:, f % 4, 0, :],
                                        ALU.subtract).then_inc(lo_done, 1)

            def recurrence(c, i):
                base = c * NL
                if i == 0:
                    dve.wait_ge(y_ready, c * 4 + 4)
                wait(dve, lif, base + i)
                if i == 0:
                    op = nc.vector.scalar_tensor_tensor(leak[:], y[:], BETA, y[:], ALU.mult, ALU.add)
                elif i == 1:
                    op = nc.vector.scalar_tensor_tensor(neg_mem[:], y[:], 1.0, leak[:], ALU.is_gt, ALU.subtract)
                elif i == 2:
                    op = nc.vector.tensor_scalar(spikes[:], y[:], 1.0, None, ALU.is_gt)
                elif i < 13:
                    kind = (i - 3) % 3
                    if kind == 0:
                        op = nc.vector.scalar_tensor_tensor(spikes[:], neg_mem[:], -1.0, spikes[:], ALU.is_lt, ALU.add)
                    elif kind == 1:
                        op = nc.vector.scalar_tensor_tensor(leak[:], neg_mem[:], -BETA, y[:], ALU.mult, ALU.add)
                    else:
                        op = nc.vector.scalar_tensor_tensor(neg_mem[:], neg_mem[:], -1.0, leak[:], ALU.is_lt, ALU.subtract)
                else:
                    dve.wait_ge(sig_done, c * 3 + 3)
                    wait(dve, gate_stored, c * 16)
                    op = nc.vector.scalar_tensor_tensor(gate[:], spikes[:], 1.0 / STEPS, leak[:], ALU.mult, ALU.mult)
                op.then_inc(lif, 1)

            def chunk(c, par, ahead=True):
                first = isinstance(c, int) and c == 0
                for f in range(FB):
                    square(c, f)
                    if f:
                        hid_lo(c, f - 1)
                    elif not first:
                        hid_lo(c - 1, FB - 1)
                    if f == 3 and not (isinstance(c, int) and c < 2):
                        recurrence(c - 2, 13)
                    if f >= 3 and not first:
                        recurrence(c - 1, f - 3)
                    if ahead and f == 1:
                        statistics(c + 1)
                    if ahead and f == 4:
                        normalise(c + 1)
                    if ahead and f in (8, 10, 12, 14):
                        part_lo(c + 1, 1 - par, (f - 8) // 2)

            statistics(0)
            normalise(0)
            for k in range(EB):
                part_lo(0, 0, k)
            chunks(dve, chunk, NC - 2)
            chunk(NC - 1, (NC - 1) % 2, ahead=False)
            hid_lo(NC - 1, FB - 1)
            recurrence(NC - 2, 13)
            for i in range(NL):
                recurrence(NC - 1, i)


HEADS = 16
HD = 32
HG = 4
S = 1024
TB = S // P
SLOT_STEPS = 16
SCALE = 512.0 ** -0.5
TW = S + 7 * P
ROWS = 3 * HD
S_TILES = {2: 3, 3: 3, 4: 3, 5: 3, 6: 2, 7: 2, 8: 3, 9: 3, 10: 3, 11: 3, 12: 2, 13: 2}


def attention(nc, d, w, NB):
    NG = 4 * NB
    with ExitStack() as ctx:
        sb = lambda name, shape, dt: ctx.enter_context(nc.sbuf_tensor(name, shape, dt))
        pt = lambda name, shape, dt: ctx.enter_context(nc.psum_tensor(name, shape, dt))
        sem = lambda name: ctx.enter_context(nc.semaphore(name))
        xT = sb("xT", [P, 2, EB, S], F16)
        toep = sb("toep", [P, 2, HG, TW], F32)
        qst = sb("qst", [P, 2, HG, S], F16)
        kst = sb("kst", [P, 2, HG, S], F16)
        nat = sb("nat", [P, 2, 2, S], F16)
        val = sb("val", [P, 2, TB, P], F32)
        prob = sb("prob", [P, 2, HG, 512], F32)
        sink = sb("sink", [P, 2, S], BF16)
        nmax = sb("nmax", [P, 2, HG, TB], F32)
        den = sb("den", [P, 2, HG, TB], F32)
        lnd = sb("lnd", [P, 2, HG, 4], F32)
        sub = sb("sub", [P, 3, HG, 4], F32)
        subT = sb("subT", [P, 2, 4, HG, HD], F16)
        identh = sb("identh", [P, P], F16)
        outT = sb("outT", [P, 2, 512], F32)
        tok = sb("tok", [P, TB, 512], F32)
        gamma = sb("gamma_row", [P, 512], F32)
        beta = sb("beta_row", [P, 512], F32)
        x_t = sb("x_t", [P, 2, 512], F32)
        g_t = sb("g_t", [P, 2, 512], F32)
        fst = sb("fst", [P, 4, 6], F32)
        fmv = sb("fmv", [P, 4, 2], F32)
        frs = sb("frs", [P, 8, 4], F32)
        s_ps = pt("s_ps", [P, 2, S], F32)
        st_ps = pt("st_ps", [P, 2, BANK], F32)
        acc = pt("acc", [P, BANK], F32)
        misc = pt("misc", [P, BANK], F32)

        consts = sem("consts")
        const_loaded = sem("const_loaded")
        xt_loaded = sem("xt_loaded")
        stacked = [sem(f"stacked{j}") for j in range(HG)]
        toep_loaded = [sem(f"toep_loaded{i}") for i in range(2)]
        qk_ps = sem("qk_ps")
        qk_hi = sem("qk_hi")
        qk_read = sem("qk_read")
        v_ps = sem("v_ps")
        v_read = sem("v_read")
        s_done = sem("s_done")
        max_done = sem("max_done")
        sum_done = sem("sum_done")
        ln_done = sem("ln_done")
        sub_step = sem("sub_step")
        rows_ps = sem("rows_ps")
        rows_read = sem("rows_read")
        st_done = sem("st_done")
        p_done = sem("p_done")
        pv_done = sem("pv_done")
        acc_read = sem("acc_read")
        tr_ps = sem("tr_ps")
        tr_read = sem("tr_read")
        fin_stat = sem("fin_stat")
        fin_log = sem("fin_log")
        fin_guess = sem("fin_guess")
        fin_newton = sem("fin_newton")
        fin_norm = sem("fin_norm")
        fin_loaded = [sem(f"fin_loaded{i}") for i in range(2)]
        fin_step = sem("fin_step")
        out_stored = sem("out_stored")
        block = ctx.enter_context(nc.Block())

        def wait(eng, s, value):
            if not (isinstance(value, int) and value <= 0):
                eng.wait_ge(s, value)

        def slots(eng, slot):
            slot(-1, 2)
            slot(-1, 3)
            for hg in range(HG):
                slot(0, hg)
            with eng.Fori(1, NB - 1) as b:
                for hg in range(HG):
                    slot(b, hg)
            for hg in range(HG):
                slot(NB - 1, hg)

        class Slot:
            def __init__(self, b, hg):
                self.b, self.hg = b, hg
                self.g = b * HG + hg
                fixed = isinstance(b, int)
                self.main = not fixed or self.g >= 0
                self.scores = not fixed or -1 <= self.g < NG - 1
                self.project = not fixed or self.g < NG - 2
                self.prev = not fixed or self.g >= 1
                self.par = hg % 2
                self.next_b, self.next_hg = (b, hg + 1) if hg < 3 else (b + 1, 0)
                self.ahead_hg = (hg + 2) % HG
                self.new_batch = hg == 2 and self.project
                self.finish0 = self.main and hg == 3
                self.finish1 = hg == 0 and (not fixed or b >= 1)

        def toep_uses(b, hg):
            return b * 2 + hg // 2 + 1

        @block.sync
        def _(sp):
            def load_xT(b):
                for part in range(2):
                    for half in range(2):
                        sp.dma_start(xT[:, part, :, half * 512:(half + 1) * 512],
                                     d["xnT"].rearrange("c a (k p) s -> c a p k s", p=P)[b * 2 + half, part]
                                     ).then_inc(xt_loaded, 16)

            def finish(b, half):
                F = b * 2 + half

                def load(t):
                    wait(sp, fin_step, (F * 4 + t - 1) * 4)
                    for dst, src in ((x_t, "x"), (g_t, "gate")):
                        sp.dma_start(dst[:, t % 2, :], d[src].rearrange("(n p) e -> n p e", p=P)[b * 8 + half * 4 + t]).then_inc(fin_loaded[t % 2], 16)

                load(0)
                load(1)
                for t in range(4):
                    sp.wait_ge(fin_step, F * 16 + t * 4 + 4)
                    sp.dma_start(d["out"].rearrange("(n p) e -> n p e", p=P)[b * 8 + half * 4 + t], tok[:, half * 4 + t, :]).then_inc(out_stored, 16)
                    if t < 2:
                        load(t + 2)

            def slot(b, hg):
                s = Slot(b, hg)
                g = s.g
                if s.scores:
                    wait(sp, st_done, g * 64)
                    sp.wait_ge(qk_read, g * 4 + 8)
                    op = 1 - s.par
                    for j in range(HG):
                        rows = slice(j * HD, (j + 1) * HD)
                        for dst, at, src, part in ((qst, 0, 0, 0), (kst, 0, 1, 0), (qst, 1, 0, 0),
                                                   (kst, 1, 1, 1), (qst, 2, 0, 1), (kst, 2, 1, 0)):
                            sp.dma_start(dst[at * HD:(at + 1) * HD, op, j, :], nat[rows, src, part, :]).then_inc(stacked[j], 16)
                    wait(sp, pv_done, g * 16)
                    pitch = d["table_rows"].shape[2]
                    src = bass.AP(tensor=d["table_rows"].tensor, offset=s.next_hg * HG * P * pitch + P - 1,
                                  ap=[[pitch - 1, P], [P * pitch, HG], [1, TW]])
                    sp.dma_start(toep[:, op], src).then_inc(toep_loaded[op], 16)
                if s.new_batch:
                    wait(sp, v_ps, g * 2 + 4)
                    load_xT(b + 1)
                if s.finish1:
                    finish(b - 1, 1)
                if s.finish0:
                    finish(b, 0)

            sp.dma_start(gamma[:], bass.AP(tensor=d["gamma"].tensor, offset=0, ap=[[0, P], [1, 512]])).then_inc(const_loaded, 16)
            sp.dma_start(beta[:], bass.AP(tensor=d["beta"].tensor, offset=0, ap=[[0, P], [1, 512]])).then_inc(const_loaded, 16)
            slots(sp, slot)
            finish(NB - 1, 1)

        @block.tensor
        def _(pe):
            last_use = [None]

            def take_misc():
                if last_use[0]:
                    pe.wait_ge(*last_use[0])

            def project_v(s, c):
                take_misc()
                for q in range(4):
                    t = c * 4 + q
                    m = 0
                    for k in range(EB):
                        for a, bb in TERMS:
                            last = nc.tensor.matmul(misc[:, q * P:(q + 1) * P], xT[:, a, k, t * P:(t + 1) * P],
                                                    w["v"][:, bb, k, s.next_hg * P:(s.next_hg + 1) * P],
                                                    start=(m == 0), stop=(m == 11))
                            m += 1
                last.then_inc(v_ps, 1)
                last_use[0] = (v_read, s.g * 2 + 2 + c + 1)

            def project_qk(s, u):
                take_misc()
                if u == 0 and s.ahead_hg == 0:
                    pe.wait_ge(xt_loaded, (s.b + 2) * 64)
                ww, c, m = w["q" if u < 2 else "k"], u % 2, 0
                for k in range(EB):
                    for a, bb in TERMS:
                        last = nc.tensor.matmul(misc[:], ww[:, a, k, s.ahead_hg * P:(s.ahead_hg + 1) * P],
                                                xT[:, bb, k, c * 512:(c + 1) * 512], start=(m == 0), stop=(m == 11))
                        m += 1
                last.then_inc(qk_ps, 1)
                last_use[0] = (qk_read, s.g * 4 + 8 + u + 1)

            def rows(s, half):
                take_misc()
                pe.wait_ge(sub_step, ((s.g + 1) * 2 + half) * 6 + 6)
                for q in range(4):
                    last = nc.tensor.matmul(misc[:, q * P:(q + 1) * P], subT[:, half, q].rearrange("p j r -> p (j r)"),
                                            identh[:], start=True, stop=True)
                last.then_inc(rows_ps, 1)
                last_use[0] = (rows_read, s.g * 2 + 2 + half + 1)

            def transpose_out(g, half):
                take_misc()
                pe.wait_ge(acc_read, g * 2 + half + 1)
                for q in range(4):
                    last = nc.tensor.transpose(misc[:, q * P:(q + 1) * P], outT[:, half, q * P:(q + 1) * P], w["ident"][:])
                last.then_inc(tr_ps, 1)
                last_use[0] = (tr_read, g * 2 + half + 1)

            def score_tile(s, i):
                n = s.g * 32 + 32 + i
                half, j, st = i // 16, i % 16 // 4, i // 16 * 4 + i % 4
                op = 1 - s.par
                if i < 16 and i % 4 == 0:
                    pe.wait_ge(stacked[j], s.g * 96 + 192)
                wait(pe, sum_done, n - 1)
                for c in range(2):
                    last = nc.tensor.matmul(s_ps[:, i % 2, c * 512:(c + 1) * 512], qst[0:ROWS, op, j, st * P:(st + 1) * P],
                                            kst[0:ROWS, op, j, c * 512:(c + 1) * 512], start=True, stop=True)
                last.then_inc(s_done, 1)

            def score_t(s, k, j):
                n = s.g * 64 + k * 4 + j
                half, tb = k // 8, k % 8
                if tb == 0 and j == 0:
                    pe.wait_ge(rows_read, s.g * 2 + half + 1)
                wait(pe, p_done, n - 1)
                nc.tensor.matmul(st_ps[:, j % 2, :], kst[:, s.par, j, tb * P:(tb + 1) * P],
                                 qst[:, s.par, j, half * 512:(half + 1) * 512], start=True, stop=True).then_inc(st_done, 1)

            def weigh(b, hg, k):
                g, par = b * HG + hg, hg % 2
                half, tb = k // 8, k % 8
                if k == 0:
                    pe.wait_ge(v_read, g * 2 + 2)
                    pe.wait_ge(toep_loaded[par], toep_uses(b, hg) * 16)
                if tb == 0:
                    wait(pe, acc_read, g * 2 + half)
                pe.wait_ge(p_done, g * 64 + k * 4 + 4)
                for source in range(2):
                    for j in range(HG):
                        at = TW - S - tb * P + half * 512
                        moving = prob[:, k % 2, j, :] if source == 0 else toep[:, par, j, at:at + 512]
                        last = nc.tensor.matmul(acc[j * HD:(j + 1) * HD, :], val[:, par, tb, j * HD:(j + 1) * HD], moving,
                                                start=(tb == 0 and source == 0), stop=(tb == 7 and source == 1))
                last.then_inc(pv_done, 1)

            def before(b, hg):
                return (b, hg - 1) if hg else (b - 1, 3)

            def slot(b, hg):
                s = Slot(b, hg)
                if s.main:
                    last_use[0] = (rows_read, s.g * 2 + 2)
                tile = 0
                for k in range(SLOT_STEPS):
                    if s.main:
                        score_t(s, k, 0)
                        score_t(s, k, 1)
                    if k and s.main:
                        weigh(b, hg, k - 1)
                    elif k == 0 and s.prev:
                        weigh(*before(b, hg), SLOT_STEPS - 1)
                    if s.main:
                        score_t(s, k, 2)
                        score_t(s, k, 3)
                    if s.scores:
                        if k in (1, 2):
                            project_v(s, k - 1)
                        for _ in range(S_TILES.get(k, 0)):
                            score_tile(s, tile)
                            tile += 1
                    if k == 3 and s.prev:
                        transpose_out(s.g - 1, 1)
                    if k == 9 and s.main:
                        transpose_out(s.g, 0)
                    if k == 10 and s.scores:
                        rows(s, 0)
                    if 10 <= k < 14 and s.project:
                        project_qk(s, k - 10)
                    if k == 15 and s.scores:
                        rows(s, 1)

            pe.wait_ge(consts, 5)
            slots(pe, slot)
            weigh(NB - 1, HG - 1, SLOT_STEPS - 1)
            transpose_out(NG - 1, 1)

        @block.scalar
        def _(act):
            def exp_t(s, k, j):
                n = s.g * 64 + k * 4 + j
                act.wait_ge(st_done, n + 1)
                wait(act, pv_done, s.g * 16 + k - 1)
                nc.scalar.activation(prob[:, k % 2, j, :], st_ps[:, j % 2, :], ACT.Exp).then_inc(p_done, 1)

            def exp_sum(s, i):
                n = s.g * 32 + 32 + i
                j, st, op = i % 16 // 4, i // 16 * 4 + i % 4, 1 - s.par
                act.wait_ge(max_done, n + 1)
                wait(act, sum_done, n - 1)
                nc.scalar.activation(sink[:, i % 2, :], s_ps[:, i % 2, :], ACT.Exp, bias=nmax[:, op, j, st:st + 1],
                                     accum_out=den[:, op, j, st:st + 1]).then_inc(sum_done, 1)

            def ln_sums(s, half):
                act.wait_ge(sum_done, s.g * 32 + 32 + half * 16 + 16)
                nc.scalar.activation(lnd[:, half], den[:, 1 - s.par, :, half * 4:half * 4 + 4], ACT.Ln).then_inc(ln_done, 1)

            def copy_acc(g, half):
                act.wait_ge(pv_done, g * 16 + half * 8 + 8)
                wait(act, tr_ps, g * 2 + half - 1)
                nc.scalar.activation(outT[:, half, :], acc[:], ACT.Copy).then_inc(acc_read, 1)

            def root(F):
                act.wait_ge(fin_stat, F * 9 + 9)
                nc.scalar.activation(frs[:, 1, :], frs[:, 0, :], ACT.Ln).then_inc(fin_log, 1)
                act.wait_ge(fin_log, F + 1)
                nc.scalar.activation(frs[:, 2, :], frs[:, 1, :], ACT.Exp, scale=-0.5).then_inc(fin_guess, 1)

            def slot(b, hg):
                s = Slot(b, hg)
                tile = 0
                for k in range(SLOT_STEPS):
                    if s.main:
                        exp_t(s, k, 0)
                        exp_t(s, k, 1)
                    if k == 0 and s.prev:
                        copy_acc(s.g - 1, 1)
                    if k == 8 and s.main:
                        copy_acc(s.g, 0)
                    if s.main:
                        exp_t(s, k, 2)
                        exp_t(s, k, 3)
                    if s.scores:
                        for _ in range(S_TILES.get(k, 0)):
                            exp_sum(s, tile)
                            tile += 1
                        if k in (7, 13):
                            ln_sums(s, k // 13)
                    if k == 11 and s.finish0:
                        root(b * 2)
                    if k == 5 and s.finish1:
                        root(b * 2 - 1)

            load_exp_ln_tables(nc, act)
            slots(act, slot)
            copy_acc(NG - 1, 1)
            root(NB * 2 - 1)

        @block.vector
        def _(dve):
            def row_max(s, i):
                n = s.g * 32 + 32 + i
                j, st, op = i % 16 // 4, i // 16 * 4 + i % 4, 1 - s.par
                dve.wait_ge(s_done, n + 1)
                nc.vector.tensor_reduce(nmax[:, op, j, st:st + 1], s_ps[:, i % 2, :], AX, ALU.max, negate=True).then_inc(max_done, 1)

            def take_v(s, c):
                dve.wait_ge(v_ps, s.g * 2 + 2 + c + 1)
                nc.vector.tensor_scalar(val[:, 1 - s.par, c * 4:c * 4 + 4, :].rearrange("p a n -> p (a n)"), misc[:],
                                        w["unscale"][:, 1:2], None, ALU.mult).then_inc(v_read, 1)

            def take_qk(s, u):
                n = s.g * 4 + 8 + u
                which, c = u // 2, u % 2
                factor = SCALE if which == 0 else 1.0
                hi = nat[:, which, 0, c * 512:(c + 1) * 512]
                if u == 0:
                    for j in range(HG):
                        wait(dve, stacked[j], s.g * 96 + 192)
                dve.wait_ge(qk_ps, n + 1)
                nc.vector.tensor_scalar(hi, misc[:], factor, None, ALU.mult).then_inc(qk_hi, 1)
                dve.wait_ge(qk_hi, n + 1)
                nc.vector.scalar_tensor_tensor(nat[:, which, 1, c * 512:(c + 1) * 512], misc[:], factor, hi,
                                               ALU.mult, ALU.subtract).then_inc(qk_read, 1)

            def subtracted(s, half):
                op = 1 - s.par
                n = (s.g + 1) * 2 + half
                base = n * 6
                dve.wait_ge(ln_done, n + 1)
                wait(dve, rows_ps, n - 1)
                wait(dve, sub_step, base)
                columns = lambda r: subT[:, half, :, :, r].rearrange("p q j -> p j q")
                nc.vector.tensor_tensor(sub[:, 0], nmax[:, op, :, half * 4:half * 4 + 4], lnd[:, half],
                                        ALU.subtract).then_inc(sub_step, 1)
                for r in range(2):
                    dve.wait_ge(sub_step, base + 2 * r + 1)
                    nc.vector.tensor_copy(columns(r), sub[:, r]).then_inc(sub_step, 1)
                    dve.wait_ge(sub_step, base + 2 * r + 2)
                    nc.vector.tensor_tensor(sub[:, r + 1], sub[:, r], columns(r), ALU.subtract).then_inc(sub_step, 1)
                dve.wait_ge(sub_step, base + 5)
                nc.vector.tensor_copy(columns(2), sub[:, 2]).then_inc(sub_step, 1)

            def take_rows(s, half):
                dve.wait_ge(rows_ps, s.g * 2 + 2 + half + 1)
                for j in range(HG):
                    last = nc.vector.tensor_copy(qst[ROWS:P, 1 - s.par, j, half * 512:(half + 1) * 512],
                                                 misc[j * HD:(j + 1) * HD, :])
                last.then_inc(rows_read, 1)

            def take_out(b, hg, half):
                g = b * HG + hg
                dve.wait_ge(tr_ps, g * 2 + half + 1)
                if hg == 0:
                    wait(dve, out_stored, (b * 2 + half - 1) * 64)
                nc.vector.tensor_copy(tok[:, half * 4:half * 4 + 4, hg * P:(hg + 1) * P],
                                      misc[:].rearrange("p (q e) -> p q e", q=4)).then_inc(tr_read, 1)

            def finish_statistics(b, half):
                F = b * 2 + half
                dve.wait_ge(tr_read, b * 8 + 7 + half)
                for t in range(4):
                    wait(dve, fin_stat, (F - 1) * 9 + t + 5)
                    nc.vector.bn_stats(fst[:, t, :], tok[:, half * 4 + t, :]).then_inc(fin_stat, 1)
                wait(dve, fin_norm, F * 4)
                dve.wait_ge(fin_stat, F * 9 + 4)
                nc.vector.memset(frs[:, 7, :], 0.0)
                for t in range(4):
                    nc.vector.bn_aggr(fmv[:, t, :], fst[:, t, :]).then_inc(fin_stat, 1)
                dve.wait_ge(fin_stat, F * 9 + 8)
                wait(dve, fin_newton, F * 4)
                nc.vector.tensor_scalar(frs[:, 0, :], fmv[:, :, 1], LN_EPS, None, ALU.add).then_inc(fin_stat, 1)

            def finish_normalise(b, half):
                F = b * 2 + half
                dve.wait_ge(fin_guess, F + 1)
                nc.vector.tensor_tensor(frs[:, 3, :], frs[:, 2, :], frs[:, 2, :], ALU.mult).then_inc(fin_newton, 1)
                dve.wait_ge(fin_newton, F * 4 + 1)
                nc.vector.tensor_tensor(frs[:, 4, :], frs[:, 3, :], frs[:, 0, :], ALU.mult).then_inc(fin_newton, 1)
                dve.wait_ge(fin_newton, F * 4 + 2)
                nc.vector.tensor_scalar(frs[:, 5, :], frs[:, 4, :], -0.5, 1.5, ALU.mult, ALU.add).then_inc(fin_newton, 1)
                dve.wait_ge(fin_newton, F * 4 + 3)
                nc.vector.tensor_tensor(frs[:, 6, :], frs[:, 5, :], frs[:, 2, :], ALU.mult).then_inc(fin_newton, 1)
                dve.wait_ge(fin_newton, F * 4 + 4)
                for t in range(4):
                    row = tok[:, half * 4 + t, :]
                    nc.vector.tensor_scalar(row, row, fmv[:, t, 0:1], frs[:, 6, t:t + 1],
                                            ALU.subtract, ALU.mult).then_inc(fin_norm, 1)

            def slot(b, hg):
                s = Slot(b, hg)
                tile = 0
                for k in range(SLOT_STEPS):
                    if s.scores:
                        if k in (1, 2):
                            take_v(s, k - 1)
                        for _ in range(S_TILES.get(k, 0)):
                            row_max(s, tile)
                            tile += 1
                    if k == 3 and s.prev:
                        take_out(*((b, hg - 1) if hg else (b - 1, 3)), 1)
                    if k == 9 and s.main:
                        take_out(b, hg, 0)
                    if k in (9, 14) and s.scores:
                        subtracted(s, k // 14)
                    if k == 10 and s.scores:
                        take_rows(s, 0)
                    if 10 <= k < 14 and s.project:
                        take_qk(s, k - 10)
                    if k == 15 and s.scores:
                        take_rows(s, 1)
                    if s.finish0 and k == 10:
                        finish_statistics(b, 0)
                    if s.finish0 and k == 12:
                        finish_normalise(b, 0)
                    if s.finish1 and k == 4:
                        finish_statistics(b - 1, 1)
                    if s.finish1 and k == 6:
                        finish_normalise(b - 1, 1)

            nc.vector.memset(kst[ROWS:P], 0.0).then_inc(consts, 1)
            nc.vector.memset(subT[:], 0.0).then_inc(consts, 1)
            nc.vector.tensor_copy(identh[:], w["ident"][:]).then_inc(consts, 1)
            dve.wait_ge(consts, 3)
            nc.vector.memset(kst[ROWS:ROWS + 3, 0], 1.0).then_inc(consts, 1)
            nc.vector.memset(kst[ROWS:ROWS + 3, 1], 1.0).then_inc(consts, 1)
            slots(dve, slot)
            take_out(NB - 1, HG - 1, 1)
            finish_statistics(NB - 1, 1)
            finish_normalise(NB - 1, 1)

        @block.gpsimd
        def _(pool):
            def finish(b, half):
                F = b * 2 + half

                for t in range(4):
                    n = F * 4 + t
                    row = tok[:, half * 4 + t, :]
                    pool.wait_ge(fin_norm, n + 1)
                    pool.wait_ge(fin_loaded[t % 2], F * 64 + t // 2 * 32 + 32)
                    for i, (other, op) in enumerate(((gamma[:], ALU.mult), (beta[:], ALU.add),
                                                     (g_t[:, t % 2, :], ALU.mult), (x_t[:, t % 2, :], ALU.add))):
                        wait(pool, fin_step, n * 4 + i)
                        nc.gpsimd.tensor_tensor(row, row, other, op).then_inc(fin_step, 1)

            def slot(b, hg):
                s = Slot(b, hg)
                if s.finish1:
                    finish(b - 1, 1)
                if s.finish0:
                    finish(b, 0)

            pool.wait_ge(const_loaded, 32)
            slots(pool, slot)
            finish(NB - 1, 1)
            pool.wait_ge(out_stored, NB * 8 * 16)


def attention_gated_by_spikes(nc, x, fcT, prT, qT, kT, vT, tableT, gamma, beta, out):
    tokens = x.shape[0]
    xnT = nc.dram_tensor("xnT", [tokens // 512, 2, EB * P, 512], F16).ap()
    gate = nc.dram_tensor("gate", [tokens, EB * P], F32).ap()
    table_ext = nc.dram_tensor("table_ext", [tableT.shape[0], 2 * S - 1], F32).ap()
    table_rows = nc.dram_tensor("table_rows", [tableT.shape[0], P, 2 * S - 1], F32).ap()
    d = dict(x=x, fcT=fcT, prT=prT, qT=qT, kT=kT, vT=vT, tableT=tableT, gamma=gamma, beta=beta,
             table_ext=table_ext, table_rows=table_rows, xnT=xnT, gate=gate, out=out)
    with ExitStack() as ctx:
        sb = lambda name, shape, dt: ctx.enter_context(nc.sbuf_tensor(name, shape, dt))
        w = {m: sb(f"w_{m}", [P, 2, EB, 512], F16) for m in "qkv"}
        w["unscale"] = sb("unscale", [P, 4], F32)
        w["ident"] = sb("ident", [P, P], F32)
        with ExitStack() as first:
            w["fc"] = first.enter_context(nc.sbuf_tensor("w_fc", [P, 2, EB, 2048], F16))
            w["pr"] = first.enter_context(nc.sbuf_tensor("w_pr", [P, 2, FB, 512], F16))
            prepare_weights(nc, d, w)
            feed_forward(nc, d, w, tokens // 512)
        attention(nc, d, w, tokens // S)


def kernel(**inputs):
    import numpy as _np
    import concourse.bacc as _bacc
    from concourse import mybir as _mybir
    from concourse.bass_utils import run_bass_kernel_spmd as _run

    laid_out = {
        "in_x": inputs["L0_attn_x"].reshape(-1, 512),
        "in_fcT": inputs["L0_ffn_W_fc"].T,
        "in_prT": inputs["L0_ffn_W_proj"].T,
        "in_qT": inputs["L0_attn_Wq"].T,
        "in_kT": inputs["L0_attn_Wk"].T,
        "in_vT": inputs["L0_attn_Wv"].T,
        "in_tableT": inputs["L0_attn_bias_table"].T,
        "in_gamma": inputs["L0_attn_ln_gamma"],
        "in_beta": inputs["L0_attn_ln_beta"],
    }
    nc = _bacc.Bacc("TRN2", target_bir_lowering=False, num_devices=1)
    arrays, args = {}, []
    for name, a in laid_out.items():
        a = _np.ascontiguousarray(a)
        arrays[name] = a
        args.append(nc.dram_tensor(name, a.shape, _mybir.dt.from_np(a.dtype), kind="ExternalInput").ap())
    tokens, width = laid_out["in_x"].shape
    args.append(nc.dram_tensor("result", (tokens, width), _mybir.dt.float32, kind="ExternalOutput").ap())
    attention_gated_by_spikes(nc, *args)
    r = _run(nc, [arrays], core_ids=[0])
    return r.results[0]["result"].reshape(inputs["L0_attn_x"].shape)
```

```python
from contextlib import ExitStack

import concourse.bass as bass
from concourse import mybir

ALU = mybir.AluOpType
ACT = mybir.ActivationFunctionType
F32 = mybir.dt.float32
F16 = mybir.dt.float16
BF16 = mybir.dt.bfloat16
I32 = mybir.dt.int32
AX = mybir.AxisListType.X
P = 128
BANK = 512
LN_EPS = 1e-5
STEPS = 5
BETA = 0.9
EXPONENT = 0x7F800000
EXP_LN_SET = 6
EB = 4
FB = 16
TERMS = ((0, 0), (0, 1), (1, 0))


def load_exp_ln_tables(nc, act):
    act.add_instruction(mybir.InstLoadActFuncSet(
        name=nc.get_next_instruction_name(), engine=mybir.EngineType.Activation,
        ins=[], outs=[], act_func_set_id=EXP_LN_SET))


def wait(eng, s, value):
    if not (isinstance(value, int) and value <= 0):
        eng.wait_ge(s, value)


class SpikingGate:

    STEPS = 14

    def __init__(self, nc, ctx, d):
        self.nc, self.d = nc, d
        sem = lambda name: ctx.enter_context(nc.semaphore(name))
        sb = lambda name, shape: ctx.enter_context(nc.sbuf_tensor(name, shape, F32))
        self.recurrence_or_probs = sb("recurrence_or_probs", [P, 4, 4, 512])
        self.gate_or_tokens = sb("gate_or_tokens", [P, 8, 512])
        self.x_or_gain = sb("x_or_gain", [P, 4, 512])
        gamma, beta = sb("gamma_row", [P, 512]), sb("beta_row", [P, 512])
        self.y, self.neg_mem, self.leak, self.spikes = (self.recurrence_or_probs[:, i] for i in range(4))
        self.gate = self.gate_or_tokens[:, 0:4]
        self.shift = self.gate_or_tokens[:, 4:8]
        self.x_again = self.x_or_gain[:]
        self.gamma, self.beta = gamma, beta
        self.y_ready = sem("y_ready")
        self.lif = sem("lif")
        self.sig_done = sem("sig_done")
        self.folded = sem("folded")
        self.norm_loaded = sem("norm_loaded")
        self.x_again_loaded = sem("x_again_loaded")
        self.gate_stored = sem("gate_stored")
        self.shift_stored = sem("shift_stored")

    def load_x(self, eng, c):
        wait(eng, self.folded, c * 3)
        eng.dma_start(self.x_again, self.d["x"].rearrange("(c t p) e -> c p t e", p=P, t=4)[c]).then_inc(self.x_again_loaded, 16)

    def store(self, eng, c):
        chunk_of = lambda name: self.d[name].rearrange("(c t p) e -> c p t e", p=P, t=4)[c]
        eng.wait_ge(self.folded, c * 3 + 2)
        eng.dma_start(chunk_of("gain"), self.gate).then_inc(self.gate_stored, 16)
        eng.wait_ge(self.folded, c * 3 + 3)
        eng.dma_start(chunk_of("shift"), self.shift).then_inc(self.shift_stored, 16)

    def recurrence(self, c, i):
        dve = self.nc.vector
        base = c * self.STEPS
        if i == 0:
            dve.wait_ge(self.y_ready, c * 4 + 4)
        wait(dve, self.lif, base + i)
        if i == 0:
            op = self.nc.vector.scalar_tensor_tensor(self.leak, self.y, BETA, self.y, ALU.mult, ALU.add)
        elif i == 1:
            op = self.nc.vector.scalar_tensor_tensor(self.neg_mem, self.y, 1.0, self.leak, ALU.is_gt, ALU.subtract)
        elif i == 2:
            op = self.nc.vector.tensor_scalar(self.spikes, self.y, 1.0, None, ALU.is_gt)
        elif i < 13:
            kind = (i - 3) % 3
            if kind == 0:
                op = self.nc.vector.scalar_tensor_tensor(self.spikes, self.neg_mem, -1.0, self.spikes, ALU.is_lt, ALU.add)
            elif kind == 1:
                op = self.nc.vector.scalar_tensor_tensor(self.leak, self.neg_mem, -BETA, self.y, ALU.mult, ALU.add)
            else:
                op = self.nc.vector.scalar_tensor_tensor(self.neg_mem, self.neg_mem, -1.0, self.leak, ALU.is_lt, ALU.subtract)
        else:
            dve.wait_ge(self.sig_done, c * 3 + 3)
            wait(dve, self.gate_stored, c * 16)
            op = self.nc.vector.scalar_tensor_tensor(self.gate, self.spikes, 1.0 / STEPS, self.leak, ALU.mult, ALU.mult)
        op.then_inc(self.lif, 1)

    def sigmoid(self, c, i):
        act = self.nc.scalar
        if i == 0:
            act.wait_ge(self.lif, c * self.STEPS + 13)
            op = self.nc.scalar.activation(self.leak, self.spikes, ACT.Exp, scale=-1.0 / STEPS)
        else:
            act.wait_ge(self.sig_done, c * 3 + i)
            if i == 1:
                op = self.nc.scalar.activation(self.leak, self.leak, ACT.Ln, bias=1.0)
            else:
                op = self.nc.scalar.activation(self.leak, self.leak, ACT.Exp, scale=-1.0)
        op.then_inc(self.sig_done, 1)

    def fold(self, c):
        pool = self.nc.gpsimd
        rows = lambda row: row[:].unsqueeze(1).broadcast_to([P, 4, 512])
        pool.wait_ge(self.lif, c * self.STEPS + self.STEPS)
        wait(pool, self.shift_stored, c * 16)
        self.nc.gpsimd.tensor_tensor(self.shift, self.gate, rows(self.beta), ALU.mult).then_inc(self.folded, 1)
        self.nc.gpsimd.tensor_tensor(self.gate, self.gate, rows(self.gamma), ALU.mult).then_inc(self.folded, 1)
        pool.wait_ge(self.x_again_loaded, c * 16 + 16)
        pool.wait_ge(self.folded, c * 3 + 1)
        self.nc.gpsimd.tensor_tensor(self.shift, self.shift, self.x_again, ALU.add).then_inc(self.folded, 1)


def prepare_weights(nc, d, w, spiking):
    with ExitStack() as ctx:
        sb = lambda name, shape, dt: ctx.enter_context(nc.sbuf_tensor(name, shape, dt))
        sem = lambda name: ctx.enter_context(nc.semaphore(name))
        stage_fc = sb("stage_fc", [P, EB, 2048], F32)
        stage_pr = spiking.recurrence_or_probs[:].rearrange("p a b n -> p (a b) n")
        stage_qkv = [spiking.gate_or_tokens[:, 0:4], spiking.gate_or_tokens[:, 4:8], spiking.x_or_gain[:]]
        square = sb("square", [P, 4, 2048], BF16)
        ones = sb("ones", [P, P], BF16)
        norms = sb("norms", [P, 8], F32)
        work = sb("work", [P, 24], F32)
        rows, known = d["tableT"].shape
        table = sb("table", [rows, d["table_ext"].shape[1]], F32)
        ps = ctx.enter_context(nc.psum_tensor("ps_norm", [P, 8, BANK], F32))

        loaded = [sem(f"loaded{n}") for n in range(11)]
        ones_set = sem("ones_set")
        ident_step = sem("ident_step")
        squared = sem("squared")
        squared_qkv = sem("squared_qkv")
        summed = sem("summed")
        summed_qkv = sem("summed_qkv")
        normed = [sem(f"normed{i}") for i in range(3)]
        rooted = [sem(f"rooted{i}") for i in range(3)]
        scale_step = [sem(f"scale_step{i}") for i in range(3)]
        inverted = sem("inverted")
        hi_done = sem("hi_done")
        lo_done = sem("lo_done")
        table_loaded = sem("table_loaded")
        table_grown = sem("table_grown")
        block = ctx.enter_context(nc.Block())

        flat = lambda t: t.rearrange("p a n -> p (a n)")
        pieces = ([stage_fc[:, k, :] for k in range(EB)]
                  + [flat(stage_pr[:, 4 * k:4 * k + 4, :]) for k in range(4)]
                  + [flat(stage_qkv[m]) for m in range(3)])
        part_of = lambda part: ([w["fc"][:, part, k, :] for k in range(EB)]
                                + [flat(w["pr"][:, part, 4 * k:4 * k + 4, :]) for k in range(4)]
                                + [flat(w[m][:, part, :, :]) for m in "qkv"])
        hi_of, lo_of = part_of(0), part_of(1)
        SCALE_FC, SCALE_PR, SCALE_Q, SCALE_K, SCALE_V = 12, 13, 14, 15, 16
        scale_of = [SCALE_FC] * 4 + [SCALE_PR] * 4 + [SCALE_Q, SCALE_K, SCALE_V]
        ORDER = (0, 1, 2, 3, 8, 9, 10, 4, 5, 6, 7)
        FC, PROJ, QKV = 0, 1, 2
        STEPS_OF = (3, 4, 6)

        @block.sync
        def _(sp):
            sources = ([d["fcT"].rearrange("(k p) n -> k p n", p=P)[k] for k in range(EB)]
                       + [d["prT"].rearrange("(k p) n -> p k n", p=P)[:, 4 * k:4 * k + 4] for k in range(4)]
                       + [d[name].rearrange("(k p) n -> p k n", p=P) for name in ("qT", "kT", "vT")])
            staged = ([stage_fc[:, k, :] for k in range(EB)] + [stage_pr[:, 4 * k:4 * k + 4] for k in range(4)]
                      + stage_qkv)
            for n in ORDER:
                sp.dma_start(staged[n], sources[n]).then_inc(loaded[n], 16)
            sp.dma_start(table[:, :known], d["tableT"]).then_inc(table_loaded, 16)
            sp.wait_ge(table_grown, 1)
            sp.dma_start(d["table_ext"], table[:]).then_inc(table_loaded, 16)
            sp.wait_ge(table_loaded, 32)

        @block.gpsimd
        def _(pool):
            nc.gpsimd.memset(w["ident"][:], 0.0).then_inc(ident_step, 1)
            pool.wait_ge(ident_step, 1)
            nc.gpsimd.affine_select(out=w["ident"][:], in_=w["ident"][:], compare_op=ALU.not_equal, fill=1.0,
                                    base=0, pattern=[[-1, P]], channel_multiplier=1).then_inc(ident_step, 1)
            for m in range(3):
                pool.wait_ge(loaded[8 + m], 16)
                if m == 2:
                    pool.wait_ge(summed_qkv, 1)
                nc.gpsimd.tensor_tensor(square[:, 2 + m % 2, :], pieces[8 + m], pieces[8 + m], ALU.mult).then_inc(squared_qkv, 1)
            pool.wait_ge(ident_step, 2)

        @block.scalar
        def _(act):
            def square_piece(n):
                act.wait_ge(loaded[n], 16)
                if n >= 2:
                    act.wait_ge(summed, n - 1)
                nc.scalar.activation(square[:, n % 2, :], pieces[n], ACT.Square).then_inc(squared, 1)

            def root(which, first, powers):
                act.wait_ge(normed[which], (2, 2, 7)[which])
                last = first + len(powers)
                nc.scalar.activation(work[:, first:last], norms[:, first:last], ACT.Ln).then_inc(rooted[which], 1)
                act.wait_ge(rooted[which], 1)
                for i, power in enumerate(powers):
                    c = first + i
                    nc.scalar.activation(work[:, c + 4:c + 5], work[:, c:c + 1], ACT.Exp, scale=power).then_inc(rooted[which], 1)

            def hi(which, pieces_of):
                act.wait_ge(scale_step[which], STEPS_OF[which])
                for n in pieces_of:
                    c = scale_of[n]
                    nc.scalar.activation(hi_of[n], pieces[n], ACT.Copy, scale=work[:, c:c + 1]).then_inc(hi_done, 1)

            load_exp_ln_tables(nc, act)
            for n in range(4):
                square_piece(n)
            root(FC, 0, (0.5,))
            hi(FC, range(4))
            square_piece(4)
            square_piece(5)
            root(QKV, 2, (0.5, 0.25))
            hi(QKV, range(8, 11))
            square_piece(6)
            square_piece(7)
            root(PROJ, 1, (0.5,))
            hi(PROJ, range(4, 8))

        @block.tensor
        def _(pe):
            def column_sums(n):
                for c in range(4):
                    if n < 4:
                        last = nc.tensor.matmul(ps[:, c, :], ones[:], square[:, n % 2, c * BANK:(c + 1) * BANK],
                                                   start=(n == 0), stop=(n == 3))
                    elif n < 8:
                        last = nc.tensor.matmul(ps[:, 4, :], ones[:], square[:, n % 2, c * BANK:(c + 1) * BANK],
                                                   start=(n == 4 and c == 0), stop=(n == 7 and c == 3))
                    else:
                        last = nc.tensor.matmul(ps[:, n - 3, :], ones[:], square[:, 2 + n % 2, c * BANK:(c + 1) * BANK],
                                                   start=(c == 0), stop=(c == 3))
                return last

            pe.wait_ge(ones_set, 1)
            for n in ORDER:
                if n < 8:
                    pe.wait_ge(squared, n + 1)
                    column_sums(n).then_inc(summed, 1)
                else:
                    pe.wait_ge(squared_qkv, n - 7)
                    column_sums(n).then_inc(summed_qkv, 1)

        @block.vector
        def _(dve):
            def largest(which, columns):
                for c, bank in columns:
                    nc.vector.tensor_reduce(norms[:, c:c + 1], bank, mybir.AxisListType.XY if which == FC else AX,
                                            ALU.max).then_inc(normed[which], 1)
                dve.wait_ge(normed[which], len(columns))
                for c, bank in columns:
                    nc.vector.tensor_scalar(norms[:, c:c + 1], norms[:, c:c + 1], 1e-18, None, ALU.max).then_inc(normed[which], 1)

            def powers_of_two(which, first, count, roots):
                step = scale_step[which]
                dve.wait_ge(rooted[which], roots)
                nc.vector.tensor_scalar(work[:, first:first + count].bitcast(I32), work[:, first - 4:first - 4 + count].bitcast(I32),
                                        EXPONENT, None, ALU.bitwise_and).then_inc(step, 1)
                dve.wait_ge(step, 1)
                nc.vector.reciprocal(work[:, first + 9:first + 9 + count], work[:, first:first + count]).then_inc(step, 1)

            def lo(first, last):
                for i in range(first, last):
                    n = ORDER[i]
                    c = scale_of[n]
                    dve.wait_ge(hi_done, i + 1)
                    nc.vector.scalar_tensor_tensor(lo_of[n], pieces[n], work[:, c:c + 1], hi_of[n],
                                                   ALU.mult, ALU.subtract).then_inc(lo_done, 1)

            nc.vector.memset(ones[:], 1.0).then_inc(ones_set, 1)
            dve.wait_ge(summed, 4)
            largest(FC, [(0, ps[:, 0:4, :])])
            powers_of_two(FC, 8, 1, 2)
            dve.wait_ge(scale_step[FC], 2)
            nc.vector.tensor_scalar(work[:, SCALE_FC:SCALE_FC + 1], work[:, 17:18], 4.0, None, ALU.mult).then_inc(scale_step[FC], 1)
            lo(0, 4)
            dve.wait_ge(summed_qkv, 3)
            largest(QKV, [(2, ps[:, 7, :]), (4, ps[:, 5, :]), (5, ps[:, 6, :])])
            dve.wait_ge(normed[QKV], 6)
            nc.vector.reciprocal(norms[:, 6:7], norms[:, 4:5]).then_inc(inverted, 1)
            dve.wait_ge(inverted, 1)
            nc.vector.tensor_tensor(norms[:, 3:4], norms[:, 5:6], norms[:, 6:7], ALU.mult).then_inc(normed[QKV], 1)
            powers_of_two(QKV, 10, 2, 3)
            nc.vector.tensor_copy(work[:, SCALE_Q:SCALE_Q + 1], work[:, 11:12]).then_inc(scale_step[QKV], 1)
            nc.vector.tensor_copy(w["unscale"][:, 1:2], work[:, 10:11]).then_inc(scale_step[QKV], 1)
            dve.wait_ge(scale_step[QKV], 2)
            nc.vector.tensor_copy(work[:, SCALE_V:SCALE_V + 1], work[:, 19:20]).then_inc(scale_step[QKV], 1)
            nc.vector.tensor_copy(work[:, SCALE_K:SCALE_K + 1], work[:, 20:21]).then_inc(scale_step[QKV], 1)
            lo(4, 7)
            dve.wait_ge(table_loaded, 16)
            nc.vector.tensor_copy(table[:, known:], table[:, known - 1:known].broadcast_to([rows, table.shape[1] - known])
                                  ).then_inc(table_grown, 1)
            dve.wait_ge(summed, 8)
            largest(PROJ, [(1, ps[:, 4, :])])
            powers_of_two(PROJ, 9, 1, 2)
            nc.vector.tensor_tensor(work[:, 21:22], work[:, 8:9], work[:, 8:9], ALU.mult).then_inc(scale_step[PROJ], 1)
            dve.wait_ge(scale_step[PROJ], 3)
            nc.vector.tensor_scalar(work[:, SCALE_PR:SCALE_PR + 1], work[:, 18:19], 256.0, None, ALU.mult).then_inc(scale_step[PROJ], 1)
            nc.vector.scalar_tensor_tensor(w["unscale"][:, 0:1], work[:, 21:22], 1.0 / (16.0 * 256.0), work[:, 9:10],
                                           ALU.mult, ALU.mult).then_inc(scale_step[PROJ], 1)
            lo(7, 11)


def feed_forward(nc, d, w, spiking, NC):
    LAG = 2
    with ExitStack() as ctx:
        sb = lambda name, shape, dt: ctx.enter_context(nc.sbuf_tensor(name, shape, dt))
        pt = lambda name, shape, dt: ctx.enter_context(nc.psum_tensor(name, shape, dt))
        sem = lambda name: ctx.enter_context(nc.semaphore(name))
        ident = w["ident"]
        y_ready, lif, norm_loaded = spiking.y_ready, spiking.lif, spiking.norm_loaded
        x_in = sb("x_in", [P, 4, 512], F32)
        xn = sb("xn", [P, 4, 512], F32)
        xnT = sb("xnT_part", [P, 2, 2, EB, 512], F16)
        stats = sb("stats", [P, 4, 6], F32)
        mv = sb("mv", [P, 4, 2], F32)
        rs = sb("rs", [P, 8, 4], F32)
        relu = sb("relu", [P, 2, 512], F32)
        hid = sb("hid", [P, 2, 512], F32)
        hid_part = sb("hid_part", [P, 4, 2, 512], F16)
        y = spiking.y
        ps_y = pt("ps_y", [P, 4, BANK], F32)
        ps_fc = pt("ps_fc", [P, 2, BANK], F32)
        ps_t = pt("ps_t", [P, 2, BANK], F32)

        x_loaded = sem("x_loaded")
        rows_stored = sem("rows_stored")
        stat_ready = sem("stat_ready")
        var_logged = sem("var_logged")
        rstd_guess = sem("rstd_guess")
        newton = sem("newton")
        xn_ready = sem("xn_ready")
        xt_ps = sem("xt_ps")
        xt_hi = sem("xt_hi")
        xt_lo = sem("xt_lo")
        xt_stored = sem("xt_stored")
        fc_done = sem("fc_done")
        relu_done = sem("relu_done")
        sq_done = sem("sq_done")
        hi_done = sem("hhi_done")
        lo_done = sem("hlo_done")
        proj_done = sem("proj_done")
        y_ps = sem("y_ps")
        block = ctx.enter_context(nc.Block())

        def chunks(eng, body, last):
            body(0, 0)
            body(1, 1)
            pairs = (last - 1) // 2
            with eng.Fori(1, pairs + 1) as i:
                body(i * 2, 0)
                body(i * 2 + 1, 1)
            for c in range(2 * pairs + 2, last + 1):
                body(c, c % 2)

        @block.sync
        def _(sp):
            def load_x(c):
                wait(sp, xn_ready, c * 4)
                sp.dma_start(x_in[:], d["x"].rearrange("(c t p) e -> c p t e", p=P, t=4)[c]).then_inc(x_loaded, 16)

            def chunk(c, par, ahead=True):
                sp.wait_ge(xt_hi, c * 4 + 4)
                sp.wait_ge(xt_lo, c * 4 + 4)
                for part in range(2):
                    sp.dma_start(d["xnT"][:, part].rearrange("c (k p) s -> c p k s", p=P)[c],
                                 xnT[:, par, part]).then_inc(xt_stored, 16)
                if ahead:
                    load_x(c + 1)
                of_chunk = lambda t: t.rearrange("(c h) p n -> c h p n", h=heads)[c]
                ext = d["table_ext"].unsqueeze(1).broadcast_to(d["table_rows"].shape)
                sp.dma_start(of_chunk(d["table_rows"]), of_chunk(ext)).then_inc(rows_stored, 16)
                if not (isinstance(c, int) and c < 2):
                    spiking.load_x(sp, c - 2)
                    spiking.store(sp, c - 2)

            heads = d["table_ext"].shape[0] // NC
            load_x(0)
            for dst, name in ((spiking.gamma, "gamma"), (spiking.beta, "beta")):
                sp.dma_start(dst[:], bass.AP(tensor=d[name].tensor, offset=0, ap=[[0, P], [1, 512]])).then_inc(norm_loaded, 16)
            chunks(sp, chunk, NC - 2)
            chunk(NC - 1, (NC - 1) % 2, ahead=False)
            sp.wait_ge(xt_stored, 32 * NC)
            sp.wait_ge(rows_stored, 16 * NC)

        @block.tensor
        def _(pe):
            def transpose(c, k):
                if k == 0:
                    pe.wait_ge(xn_ready, c * 4 + 4)
                n = c * 4 + k
                wait(pe, xt_hi, n - 1)
                wait(pe, xt_lo, n - 1)
                for t in range(4):
                    last = nc.tensor.transpose(ps_t[:, k % 2, t * P:(t + 1) * P], xn[:, t, k * P:(k + 1) * P], ident[:])
                last.then_inc(xt_ps, 1)

            def fc(c, par, f):
                n = c * FB + f
                if f == 0:
                    pe.wait_ge(xt_lo, c * 4 + 4)
                    pe.wait_ge(xt_hi, c * 4 + 4)
                wait(pe, relu_done, n - 1)
                m = 0
                for k in range(EB):
                    for a, b in TERMS:
                        last = nc.tensor.matmul(ps_fc[:, f % 2, :], w["fc"][:, a, k, f * P:(f + 1) * P],
                                                xnT[:, par, b, k, :], start=(m == 0), stop=(m == 11))
                        m += 1
                last.then_inc(fc_done, 1)

            def proj(c, f):
                n = c * FB + f
                pe.wait_ge(lo_done, n + 1)
                pe.wait_ge(hi_done, n + 1)
                for t in range(4):
                    if f == 0:
                        wait(pe, y_ready, (c - 1) * 4 + t + 1)
                    for m, (a, b) in enumerate(TERMS):
                        last = nc.tensor.matmul(ps_y[:, t, :], hid_part[:, f % 4, a, t * P:(t + 1) * P],
                                                w["pr"][:, b, f, :], start=(f == 0 and m == 0), stop=(f == FB - 1 and m == 2))
                    if f == FB - 1:
                        last.then_inc(y_ps, 1)
                    elif t == 3:
                        last.then_inc(proj_done, 1)

            def chunk(c, par, ahead=True):
                for f in range(FB):
                    fc(c, par, f)
                    if f >= LAG:
                        proj(c, f - LAG)
                    elif not (isinstance(c, int) and c == 0):
                        proj(c - 1, FB + f - LAG)
                    if ahead and f in (6, 8, 10, 12):
                        transpose(c + 1, (f - 6) // 2)

            for k in range(EB):
                transpose(0, k)
            chunks(pe, chunk, NC - 2)
            chunk(NC - 1, (NC - 1) % 2, ahead=False)
            for f in range(FB - LAG, FB):
                proj(NC - 1, f)

        def hidden_free(eng, c, f):
            if f >= 4:
                wait(eng, proj_done, c * (FB - 1) + f - 3)
            elif f < 3:
                wait(eng, proj_done, (c - 1) * (FB - 1) + f + FB - 3)
            else:
                wait(eng, y_ps, c * 4)

        @block.scalar
        def _(act):
            def root(c):
                act.wait_ge(stat_ready, c * 9 + 9)
                nc.scalar.activation(rs[:, 1, :], rs[:, 0, :], ACT.Ln).then_inc(var_logged, 1)
                act.wait_ge(var_logged, c + 1)
                nc.scalar.activation(rs[:, 2, :], rs[:, 1, :], ACT.Exp, scale=-0.5).then_inc(rstd_guess, 1)

            def part_hi(c, par, k):
                act.wait_ge(xt_ps, c * 4 + k + 1)
                if k == 0:
                    wait(act, xt_stored, (c - 1) * 32)
                nc.scalar.activation(xnT[:, par, 0, k, :], ps_t[:, k % 2, :], ACT.Copy).then_inc(xt_hi, 1)

            def hid_hi(c, f):
                n = c * FB + f
                act.wait_ge(sq_done, n + 1)
                hidden_free(act, c, f)
                nc.scalar.activation(hid_part[:, f % 4, 0, :], hid[:, f % 2, :], ACT.Copy).then_inc(hi_done, 1)

            def chunk(c, par, ahead=True):
                first = isinstance(c, int) and c == 0
                for f in range(FB):
                    n = c * FB + f
                    if f:
                        hid_hi(c, f - 1)
                    elif not first:
                        hid_hi(c - 1, FB - 1)
                    if f == 2 and not first:
                        copy_y(c - 1)
                    act.wait_ge(fc_done, n + 1)
                    wait(act, sq_done, n - 1)
                    nc.scalar.activation(relu[:, f % 2, :], ps_fc[:, f % 2, :], ACT.Relu).then_inc(relu_done, 1)
                    if f < 3 and not (isinstance(c, int) and c < 2):
                        spiking.sigmoid(c - 2, f)
                    if ahead and f == 2:
                        root(c + 1)
                    if ahead and f in (7, 9, 11, 13):
                        part_hi(c + 1, 1 - par, (f - 7) // 2)

            def copy_y(c):
                wait(act, lif, (c - 1) * spiking.STEPS + 11)
                for t in range(4):
                    act.wait_ge(y_ps, c * 4 + t + 1)
                    nc.scalar.activation(y[:, t, :], ps_y[:, t, :], ACT.Copy, scale=w["unscale"][:, 0:1]).then_inc(y_ready, 1)

            load_exp_ln_tables(nc, act)
            root(0)
            for k in range(EB):
                part_hi(0, 0, k)
            chunks(act, chunk, NC - 2)
            chunk(NC - 1, (NC - 1) % 2, ahead=False)
            hid_hi(NC - 1, FB - 1)
            copy_y(NC - 1)

        @block.gpsimd
        def _(pool):
            pool.wait_ge(norm_loaded, 32)
            spiking.fold(0)
            spiking.fold(1)
            with pool.Fori(1, NC // 2 - 1) as i:
                spiking.fold(i * 2)
                spiking.fold(i * 2 + 1)

        @block.vector
        def _(dve):
            def statistics(c):
                dve.wait_ge(x_loaded, c * 16 + 16)
                for t in range(4):
                    wait(dve, stat_ready, (c - 1) * 9 + t + 5)
                    nc.vector.bn_stats(stats[:, t, :], x_in[:, t, :]).then_inc(stat_ready, 1)
                wait(dve, xn_ready, c * 4)
                dve.wait_ge(stat_ready, c * 9 + 4)
                nc.vector.memset(rs[:, 7, :], 0.0)
                for t in range(4):
                    nc.vector.bn_aggr(mv[:, t, :], stats[:, t, :]).then_inc(stat_ready, 1)
                dve.wait_ge(stat_ready, c * 9 + 8)
                wait(dve, newton, c * 4)
                nc.vector.tensor_scalar(rs[:, 0, :], mv[:, :, 1], LN_EPS, None, ALU.add).then_inc(stat_ready, 1)

            def normalise(c):
                dve.wait_ge(rstd_guess, c + 1)
                nc.vector.tensor_tensor(rs[:, 3, :], rs[:, 2, :], rs[:, 2, :], ALU.mult).then_inc(newton, 1)
                dve.wait_ge(newton, c * 4 + 1)
                nc.vector.tensor_tensor(rs[:, 4, :], rs[:, 3, :], rs[:, 0, :], ALU.mult).then_inc(newton, 1)
                dve.wait_ge(newton, c * 4 + 2)
                nc.vector.tensor_scalar(rs[:, 5, :], rs[:, 4, :], -0.5, 1.5, ALU.mult, ALU.add).then_inc(newton, 1)
                dve.wait_ge(newton, c * 4 + 3)
                nc.vector.tensor_tensor(rs[:, 6, :], rs[:, 5, :], rs[:, 2, :], ALU.mult).then_inc(newton, 1)
                dve.wait_ge(newton, c * 4 + 4)
                wait(dve, xt_ps, c * 4)
                for t in range(4):
                    nc.vector.tensor_scalar(xn[:, t, :], x_in[:, t, :], mv[:, t, 0:1], rs[:, 6, t:t + 1],
                                            ALU.subtract, ALU.mult).then_inc(xn_ready, 1)

            def part_lo(c, par, k):
                dve.wait_ge(xt_hi, c * 4 + k + 1)
                nc.vector.tensor_tensor(xnT[:, par, 1, k, :], ps_t[:, k % 2, :], xnT[:, par, 0, k, :],
                                        ALU.subtract).then_inc(xt_lo, 1)

            def square(c, f):
                n = c * FB + f
                dve.wait_ge(relu_done, n + 1)
                wait(dve, hi_done, n - 1)
                wait(dve, lo_done, n - 1)
                nc.vector.tensor_tensor(hid[:, f % 2, :], relu[:, f % 2, :], relu[:, f % 2, :], ALU.mult).then_inc(sq_done, 1)

            def hid_lo(c, f):
                n = c * FB + f
                dve.wait_ge(hi_done, n + 1)
                nc.vector.tensor_tensor(hid_part[:, f % 4, 1, :], hid[:, f % 2, :], hid_part[:, f % 4, 0, :],
                                        ALU.subtract).then_inc(lo_done, 1)

            def chunk(c, par, ahead=True):
                first = isinstance(c, int) and c == 0
                for f in range(FB):
                    square(c, f)
                    if f:
                        hid_lo(c, f - 1)
                    elif not first:
                        hid_lo(c - 1, FB - 1)
                    if f == 3 and not (isinstance(c, int) and c < 2):
                        spiking.recurrence(c - 2, 13)
                    if f >= 3 and not first:
                        spiking.recurrence(c - 1, f - 3)
                    if ahead and f == 1:
                        statistics(c + 1)
                    if ahead and f == 4:
                        normalise(c + 1)
                    if ahead and f in (8, 10, 12, 14):
                        part_lo(c + 1, 1 - par, (f - 8) // 2)

            statistics(0)
            normalise(0)
            for k in range(EB):
                part_lo(0, 0, k)
            chunks(dve, chunk, NC - 2)
            chunk(NC - 1, (NC - 1) % 2, ahead=False)
            hid_lo(NC - 1, FB - 1)


HEADS = 16
HD = 32
HG = 4
S = 1024
TB = S // P
SLOT_STEPS = 16
SCALE = 512.0 ** -0.5
TW = S
TABLE_COLS = S - 1 + P
ROWS = 3 * HD
TILE_LAG = 3
PARTS = 3
QK_PARTS = (0, 5, 7, 12)
V_PARTS = (0, 20, 28, 48)
SUBTRACTED = 3
V_HALVES = (1, 5)
QK_HALVES = (15, 19, 23, 27)
FINISH_OPS = {1: (1, 2), 2: (3,), 3: (4,), 9: (5, 6, 7), 10: (8, 9, 10), 11: (11, 12, 13), 12: (14, 15)}
CONSTS = 4 + TB - 1
RECURRENCES = {(-2, 17): (0, 1), (-2, 19): (2, 3), (-2, 23): (4, 5), (-2, 27): (6, 7), (-2, 31): (8,),
               (-1, 0): (9,), (-1, 2): (10,), (-1, 4): (11,), (-1, 5): (12,), (-1, 12): (13,)}
PROBS = 4


def attention(nc, d, w, spiking, NB):
    NG = 4 * NB
    NC = 2 * NB
    with ExitStack() as ctx:
        sb = lambda name, shape, dt: ctx.enter_context(nc.sbuf_tensor(name, shape, dt))
        pt = lambda name, shape, dt: ctx.enter_context(nc.psum_tensor(name, shape, dt))
        sem = lambda name: ctx.enter_context(nc.semaphore(name))
        xT = sb("xT", [P, 2, EB, S], F16)
        toep = sb("toep", [P, 2, HG, TW], F32)
        qst = sb("qst", [P, 2, HG, S], F16)
        kst = sb("kst", [P, 2, HG, S], F16)
        nat = sb("nat", [P, 2, 2, S], F16)
        val = sb("val", [P, 2, TB, P], F32)
        prob = spiking.recurrence_or_probs
        sink = sb("sink", [P, 2, S], BF16)
        nmax = sb("nmax", [P, 2, HG, TB], F32)
        den = sb("den", [P, 2, HG, TB], F32)
        lnd = sb("lnd", [P, 2, HG, 4], F32)
        sub = sb("sub", [P, 3, HG, 4], F32)
        subT = sb("subT", [P, 2, 4, HG, HD], F16)
        sub_rows = sb("sub_rows", [P, 2, 512], F16)
        identh = sb("identh", [P, P], F16)
        outT = sb("outT", [P, 2, 512], F32)
        tok = spiking.gate_or_tokens
        before_key = sb("before_key", [P, TB, TB], F32)
        far = sb("far", [P, HG], F32)
        prefix = sb("prefix", [P, 2, TB], F32)
        gain_t = spiking.x_or_gain
        shift_t = sb("shift_t", [P, 4, 512], F32)
        fst = sb("fst", [P, 4, 6], F32)
        fmv = sb("fmv", [P, 4, 2], F32)
        frs = sb("frs", [P, 8, 4], F32)
        s_ps = pt("s_ps", [P, 2, S], F32)
        st_ps = pt("st_ps", [P, 2, BANK], F32)
        acc = pt("acc", [P, BANK], F32)
        misc = pt("misc", [P, BANK], F32)

        consts = sem("consts")
        const_loaded = sem("const_loaded")
        xt_loaded = [sem(f"xt_loaded{i}") for i in range(2)]
        stacked = [sem(f"stacked{j}") for j in range(HG)]
        toep_loaded = [sem(f"toep_loaded{i}") for i in range(2)]
        qk_ps = sem("qk_ps")
        qk_hi = sem("qk_hi")
        qk_read = sem("qk_read")
        v_ps = sem("v_ps")
        v_read = sem("v_read")
        s_done = sem("s_done")
        max_done = sem("max_done")
        sum_done = sem("sum_done")
        ln_done = sem("ln_done")
        sub_step = sem("sub_step")
        rows_ps = sem("rows_ps")
        rows_read = sem("rows_read")
        rows_loaded = [sem(f"rows_loaded{i}") for i in range(2)]
        st_done = sem("st_done")
        p_done = sem("p_done")
        pv_done = sem("pv_done")
        add_dve = sem("add_dve")
        add_pool = sem("add_pool")
        pre_ps = sem("pre_ps")
        pre_read = sem("pre_read")
        acc_read = sem("acc_read")
        tr_ps = sem("tr_ps")
        tr_read = sem("tr_read")
        fin_stat = sem("fin_stat")
        fin_log = sem("fin_log")
        fin_guess = sem("fin_guess")
        fin_newton = sem("fin_newton")
        fin_norm = sem("fin_norm")
        fin_loaded = [sem(f"fin_loaded{i}") for i in range(4)]
        fin_step = sem("fin_step")
        out_stored = [sem(f"out_stored{i}") for i in range(2)]
        block = ctx.enter_context(nc.Block())

        def slots(eng, slot):
            slot(-1, 2)
            slot(-1, 3)
            for hg in range(HG):
                slot(0, hg)
            with eng.Fori(1, NB - 1) as b:
                for hg in range(HG):
                    slot(b, hg)
            for hg in range(HG):
                slot(NB - 1, hg)

        class Slot:
            def __init__(self, b, hg):
                self.b, self.hg = b, hg
                self.g = b * HG + hg
                fixed = isinstance(b, int)
                self.main = not fixed or self.g >= 0
                self.scores = not fixed or -1 <= self.g < NG - 1
                self.project = not fixed or self.g < NG - 2
                self.prev = not fixed or self.g >= 1
                self.par = hg % 2
                self.next_b, self.next_hg = (b, hg + 1) if hg < 3 else (b + 1, 0)
                self.ahead_hg = (hg + 2) % HG
                self.new_batch = hg == 2 and self.project

                self.finish0 = self.main and hg == 3
                self.finish1 = hg == 0 and (not fixed or b >= 1)

            def tiles(self, k):
                if k < TILE_LAG:
                    return (self.g, self.par, 2 * (k + SLOT_STEPS - TILE_LAG)) if self.main else None
                return (self.g + 1, 1 - self.par, 2 * (k - TILE_LAG)) if self.scores else None

            def tile_before(self, k):
                if k:
                    t = self.tiles(k - 1)
                else:
                    fixed = isinstance(self.b, int)
                    t = (self.g, self.par, 2 * (SLOT_STEPS - 1 - TILE_LAG)) if not fixed or 0 <= self.g else None
                return t and (t[0], t[1], t[2] + 1)

        def toep_uses(b, hg):
            return b * 2 + hg // 2 + 1

        def before(b, hg):
            return (b, hg - 1) if hg else (b - 1, 3)

        def bias_width(k):
            return min(512, (k % 8 + 1) * P - k // 8 * 512)

        def add_count(g, k):
            return g * 12 + (k + 1 if k < 8 else k - 3)

        def add_bias(eng, unit, heads, done, b, hg, k):
            width, par = bias_width(k), hg % 2
            if width <= 0:
                return
            at = TW - P - k % 8 * P + k // 8 * 512
            if k == 0:
                eng.wait_ge(toep_loaded[par], toep_uses(b, hg) * 16)
            eng.wait_ge(p_done, (b * HG + hg) * 64 + k * 4 + heads.stop)
            tile = prob[:, k % PROBS, heads, :width]
            unit.tensor_tensor(tile, tile, toep[:, par, heads, at:at + width], ALU.add).then_inc(done, 1)

        DVE_HEADS, POOL_HEADS = slice(0, 1), slice(1, HG)

        @block.sync
        def _(sp):
            tiles = lambda name: d[name].rearrange("(n p) e -> n p e", p=P)

            def load_xT(b):
                for half in range(2):
                    wait(sp, xt_loaded[half], b * 32)
                    for part in range(2):
                        sp.dma_start(xT[:, part, :, half * 512:(half + 1) * 512],
                                     d["xnT"].rearrange("c a (k p) s -> c a p k s", p=P)[b * 2 + half, part]
                                     ).then_inc(xt_loaded[half], 16)

            def load_tile(b, i):
                wait(sp, fin_step, (b * TB + i - 3) * 2)
                for dst, name in ((gain_t, "gain"), (shift_t, "shift")):
                    sp.dma_start(dst[:, i % 4, :], tiles(name)[b * TB + i]).then_inc(fin_loaded[i % 4], 16)

            def store_tile(b, i):
                sp.wait_ge(fin_step, (b * TB + i) * 2 + 2)
                sp.dma_start(tiles("out")[b * TB + i], tok[:, i, :]).then_inc(out_stored[i // 4], 16)
                if i < TB - 4:
                    load_tile(b, i + 4)

            def load_toep(s):
                wait(sp, add_dve, s.g * 12)
                wait(sp, add_pool, s.g * 12)
                op = 1 - s.par
                pitch = d["table_rows"].shape[2]
                src = bass.AP(tensor=d["table_rows"].tensor, offset=s.next_hg * HG * P * pitch + P - 1,
                              ap=[[pitch - 1, P], [P * pitch, HG], [1, TW]])
                sp.dma_start(toep[:, op], src).then_inc(toep_loaded[op], 16)

            def load_rows(G, par, half):
                sp.wait_ge(rows_read, G * 2 + half + 1)
                for j in range(HG):
                    sp.dma_start(qst[ROWS:ROWS + SUBTRACTED, par, j, half * 512:(half + 1) * 512],
                                 sub_rows[j * HD:j * HD + SUBTRACTED, half, :]).then_inc(rows_loaded[half], 16)

            def slot(b, hg):
                s = Slot(b, hg)
                g = s.g
                op = 1 - s.par
                if s.scores:
                    wait(sp, st_done, g * 64)
                    sp.wait_ge(qk_read, g * 4 + 8)
                    for j in range(HG):
                        rows = slice(j * HD, (j + 1) * HD)
                        for dst, at, src, part in ((qst, 0, 0, 0), (kst, 0, 1, 0), (qst, 1, 0, 0),
                                                   (kst, 1, 1, 1), (qst, 2, 0, 1), (kst, 2, 1, 0)):
                            sp.dma_start(dst[at * HD:(at + 1) * HD, op, j, :], nat[rows, src, part, :]).then_inc(stacked[j], 16)
                if s.new_batch and s.scores:
                    load_toep(s)
                    wait(sp, v_ps, g * 2 + 4)
                    load_xT(b + 1)
                elif s.new_batch:
                    load_xT(b + 1)
                    spiking.load_x(sp, NC - 2)
                    spiking.store(sp, NC - 2)
                    spiking.load_x(sp, NC - 1)
                elif s.scores:
                    load_toep(s)
                if hg == 3 and s.main:
                    if isinstance(b, int) and b == 0:
                        sp.wait_ge(spiking.gate_stored, NC * 16)
                        sp.wait_ge(spiking.shift_stored, NC * 16)
                        sp.wait_ge(spiking.folded, NC * 3)
                    for i in range(4):
                        load_tile(b, i)
                if hg == 0 and s.prev:
                    store_tile(b - 1, 0)
                    store_tile(b - 1, 1)
                if s.main:
                    load_rows(g, s.par, 1)
                if hg == 0 and s.prev:
                    for i in range(2, TB):
                        store_tile(b - 1, i)
                if s.scores:
                    load_rows(g + 1, op, 0)
                if isinstance(g, int) and g == -1:
                    spiking.store(sp, NC - 1)

            for j in range(HG):
                known = d["tableT"].shape[1]
                sp.dma_start(far[j * HD:(j + 1) * HD, :], bass.AP(tensor=d["tableT"].tensor, offset=j * known + known - 1,
                                                                 ap=[[0, HD], [HG * known, HG]]),
                             allow_slow_non_contiguous=True).then_inc(const_loaded, 16)
            slots(sp, slot)
            for i in range(TB):
                store_tile(NB - 1, i)
            for half in range(2):
                sp.wait_ge(out_stored[half], NB * 64)

        @block.tensor
        def _(pe):
            last_use = [None]

            def take_misc():
                if last_use[0]:
                    pe.wait_ge(*last_use[0])

            def project_v(s, c, part):
                if part == 0:
                    take_misc()
                terms = [(q, k, a, bb) for q in range(4) for k in range(EB) for a, bb in TERMS]
                for n in range(V_PARTS[part], V_PARTS[part + 1]):
                    q, k, a, bb = terms[n]
                    t = c * 4 + q
                    last = nc.tensor.matmul(misc[:, q * P:(q + 1) * P], xT[:, a, k, t * P:(t + 1) * P],
                                            w["v"][:, bb, k, s.next_hg * P:(s.next_hg + 1) * P],
                                            start=(n % 12 == 0), stop=(n % 12 == 11))
                if part == PARTS - 1:
                    last.then_inc(v_ps, 1)
                    last_use[0] = (v_read, s.g * 2 + 2 + c + 1)

            def project_qk(s, u, part):
                if part == 0:
                    take_misc()
                    if u < 2 and s.ahead_hg == 0:
                        pe.wait_ge(xt_loaded[u], (s.b + 2) * 32)
                ww, c = w["q" if u < 2 else "k"], u % 2
                terms = [(k, a, bb) for k in range(EB) for a, bb in TERMS]
                for n in range(QK_PARTS[part], QK_PARTS[part + 1]):
                    k, a, bb = terms[n]
                    last = nc.tensor.matmul(misc[:], ww[:, a, k, s.ahead_hg * P:(s.ahead_hg + 1) * P],
                                            xT[:, bb, k, c * 512:(c + 1) * 512], start=(n == 0), stop=(n == 11))
                if part == PARTS - 1:
                    last.then_inc(qk_ps, 1)
                    last_use[0] = (qk_read, s.g * 4 + 8 + u + 1)

            def sum_values(s):
                take_misc()
                pe.wait_ge(v_read, s.g * 2 + 4)
                for t in range(TB - 1):
                    last = nc.tensor.matmul(misc[:, :TB], val[:, 1 - s.par, t, :], before_key[:, t, :],
                                            start=(t == 0), stop=(t == TB - 2))
                last.then_inc(pre_ps, 1)
                last_use[0] = (pre_read, s.g + 2)

            def rows(G, half):
                take_misc()
                pe.wait_ge(sub_step, (G * 2 + half) * 6 + 6)
                for q in range(4):
                    last = nc.tensor.matmul(misc[:, q * P:(q + 1) * P], subT[:, half, q].rearrange("p j r -> p (j r)"),
                                            identh[:], start=True, stop=True)
                last.then_inc(rows_ps, 1)
                last_use[0] = (rows_read, G * 2 + half + 1)

            def transpose_out(g, half):
                take_misc()
                pe.wait_ge(acc_read, g * 2 + half + 1)
                for q in range(4):
                    last = nc.tensor.transpose(misc[:, q * P:(q + 1) * P], outT[:, half, q * P:(q + 1) * P], w["ident"][:])
                last.then_inc(tr_ps, 1)
                last_use[0] = (tr_read, g * 2 + half + 1)

            def score_tile(G, par, i):
                n = G * 32 + i
                j, st = i % 16 // 4, i // 16 * 4 + i % 4
                if i < 16 and i % 4 == 0:
                    pe.wait_ge(stacked[j], G * 96 + 96)
                wait(pe, sum_done, n - 1)
                for c in range(2):
                    last = nc.tensor.matmul(s_ps[:, i % 2, c * 512:(c + 1) * 512], qst[0:ROWS, par, j, st * P:(st + 1) * P],
                                            kst[0:ROWS, par, j, c * 512:(c + 1) * 512], start=True, stop=True)
                last.then_inc(s_done, 1)

            def score_t(s, k, j):
                n = s.g * 64 + k * 4 + j
                half, tb = k // 8, k % 8
                if tb == 0 and j == 0:
                    pe.wait_ge(rows_loaded[half], s.g * 64 + 64)
                wait(pe, p_done, n - 1)
                nc.tensor.matmul(st_ps[:, j % 2, :], kst[:ROWS + SUBTRACTED, s.par, j, tb * P:(tb + 1) * P],
                                 qst[:ROWS + SUBTRACTED, s.par, j, half * 512:(half + 1) * 512], start=True, stop=True).then_inc(st_done, 1)

            def weigh(b, hg, k, pair):
                g, par = b * HG + hg, hg % 2
                tb = k % 8
                if pair == 0:
                    if k == 0:
                        pe.wait_ge(v_read, g * 2 + 2)
                    if tb == 0:
                        wait(pe, acc_read, g * 2 + k // 8)
                    pe.wait_ge(p_done, g * 64 + k * 4 + 4)
                    if bias_width(k) > 0:
                        pe.wait_ge(add_dve, add_count(g, k))
                        pe.wait_ge(add_pool, add_count(g, k))
                for j in (2 * pair, 2 * pair + 1):
                    last = nc.tensor.matmul(acc[j * HD:(j + 1) * HD, :], val[:, par, tb, j * HD:(j + 1) * HD],
                                            prob[:, k % PROBS, j, :], start=(tb == 0), stop=(tb == 7))
                if pair:
                    last.then_inc(pv_done, 1)

            def between(s, h):
                for c, first in enumerate(V_HALVES):
                    if first <= h < first + PARTS and s.scores:
                        project_v(s, c, h - first)
                if h == 10 and s.main:
                    rows(s.g, 1)
                if h == 11 and s.prev:
                    transpose_out(s.g - 1, 1)
                if h == 13 and s.scores:
                    sum_values(s)
                for u, first in enumerate(QK_HALVES):
                    if first <= h < first + PARTS and s.project:
                        project_qk(s, u, h - first)
                if h == 22 and s.main:
                    transpose_out(s.g, 0)
                if h == 26 and s.scores:
                    rows(s.g + 1, 0)

            def slot(b, hg):
                s = Slot(b, hg)
                last_use[0] = ((qk_read, s.g * 4 + 8) if s.scores else (rows_read, s.g * 2 + 1) if s.main else None)
                for h in range(2 * SLOT_STEPS):
                    k, second = h // 2, h % 2
                    tiles = s.tiles(k)
                    if s.main:
                        score_t(s, k, 2 * second)
                        score_t(s, k, 2 * second + 1)
                    if tiles:
                        score_tile(tiles[0], tiles[1], tiles[2] + second)
                    if s.main and k >= 2:
                        weigh(b, hg, k - 2, second)
                    elif s.prev and k < 2:
                        weigh(*before(b, hg), SLOT_STEPS - 2 + k, second)
                    between(s, h)

            pe.wait_ge(consts, CONSTS)
            slots(pe, slot)
            for k in (SLOT_STEPS - 2, SLOT_STEPS - 1):
                weigh(NB - 1, HG - 1, k, 0)
                weigh(NB - 1, HG - 1, k, 1)
            transpose_out(NG - 1, 1)

        @block.scalar
        def _(act):
            def exp_t(s, k, j):
                n = s.g * 64 + k * 4 + j
                act.wait_ge(st_done, n + 1)
                wait(act, pv_done, s.g * SLOT_STEPS + k - PROBS + 1)
                nc.scalar.activation(prob[:, k % PROBS, j, :], st_ps[:, j % 2, :], ACT.Exp).then_inc(p_done, 1)

            def exp_sum(G, par, i):
                n = G * 32 + i
                j, st = i % 16 // 4, i // 16 * 4 + i % 4
                act.wait_ge(max_done, n + 1)
                wait(act, sum_done, n - 1)
                nc.scalar.activation(sink[:, i % 2, :], s_ps[:, i % 2, :], ACT.Exp, bias=nmax[:, par, j, st:st + 1],
                                     accum_out=den[:, par, j, st:st + 1]).then_inc(sum_done, 1)

            def ln_sums(G, par, half):
                act.wait_ge(sum_done, G * 32 + half * 16 + 16)
                nc.scalar.activation(lnd[:, half], den[:, par, :, half * 4:half * 4 + 4], ACT.Ln).then_inc(ln_done, 1)

            def root(F):
                act.wait_ge(fin_stat, F * 9 + 9)
                nc.scalar.activation(frs[:, 1, :], frs[:, 0, :], ACT.Ln).then_inc(fin_log, 1)
                act.wait_ge(fin_log, F + 1)
                nc.scalar.activation(frs[:, 2, :], frs[:, 1, :], ACT.Exp, scale=-0.5).then_inc(fin_guess, 1)

            def slot(b, hg):
                s = Slot(b, hg)
                if isinstance(s.g, int) and s.g == 0:
                    act.wait_ge(spiking.lif, NC * spiking.STEPS)
                for k in range(SLOT_STEPS):
                    if isinstance(s.g, int) and s.g == -1 and 3 <= k < 6:
                        spiking.sigmoid(NC - 1, k - 3)
                    if s.main:
                        exp_t(s, k, 0)
                        exp_t(s, k, 1)
                    if s.tile_before(k):
                        exp_sum(*s.tile_before(k))
                    if k == 3 and s.main:
                        ln_sums(s.g, s.par, 1)
                    if k == 11 and s.scores:
                        ln_sums(s.g + 1, 1 - s.par, 0)
                    if s.main:
                        exp_t(s, k, 2)
                        exp_t(s, k, 3)
                    if s.tiles(k):
                        exp_sum(*s.tiles(k))
                    if k == 13 and s.finish0:
                        root(b * 2)
                    if k == 8 and s.finish1:
                        root(b * 2 - 1)

            load_exp_ln_tables(nc, act)
            for i in range(3):
                spiking.sigmoid(NC - 2, i)
            slots(act, slot)
            root(NB * 2 - 1)

        @block.vector
        def _(dve):
            def row_max(G, par, i):
                n = G * 32 + i
                j, st = i % 16 // 4, i // 16 * 4 + i % 4
                dve.wait_ge(s_done, n + 1)
                nc.vector.tensor_reduce(nmax[:, par, j, st:st + 1], s_ps[:, i % 2, :], AX, ALU.max, negate=True).then_inc(max_done, 1)

            def take_v(s, c):
                dve.wait_ge(v_ps, s.g * 2 + 2 + c + 1)
                nc.vector.tensor_scalar(val[:, 1 - s.par, c * 4:c * 4 + 4, :].rearrange("p a n -> p (a n)"), misc[:],
                                        w["unscale"][:, 1:2], None, ALU.mult).then_inc(v_read, 1)

            def take_values(s):
                dve.wait_ge(pre_ps, s.g + 2)
                nc.vector.tensor_scalar(prefix[:, 1 - s.par, :], misc[:, :TB], far[:, s.next_hg:s.next_hg + 1], None,
                                        ALU.mult).then_inc(pre_read, 1)

            def copy_acc(g, par, half):
                dve.wait_ge(pv_done, g * 16 + half * 8 + 8)
                dve.wait_ge(pre_read, g + 1)
                wait(dve, tr_ps, g * 2 + half - 1)
                nc.vector.tensor_tensor(outT[:, half, :].rearrange("p (q n) -> p q n", q=4),
                                        acc[:].rearrange("p (q n) -> p q n", q=4),
                                        prefix[:, par, half * 4:half * 4 + 4].unsqueeze(2).broadcast_to([P, 4, P]),
                                        ALU.add).then_inc(acc_read, 1)

            def take_qk(g, u):
                n = g * 4 + 8 + u
                which, c = u // 2, u % 2
                factor = SCALE if which == 0 else 1.0
                hi = nat[:, which, 0, c * 512:(c + 1) * 512]
                if u == 0:
                    for j in range(HG):
                        wait(dve, stacked[j], g * 96 + 192)
                dve.wait_ge(qk_ps, n + 1)
                nc.vector.tensor_scalar(hi, misc[:], factor, None, ALU.mult).then_inc(qk_hi, 1)
                dve.wait_ge(qk_hi, n + 1)
                nc.vector.scalar_tensor_tensor(nat[:, which, 1, c * 512:(c + 1) * 512], misc[:], factor, hi,
                                               ALU.mult, ALU.subtract).then_inc(qk_read, 1)

            def subtracted(G, par, half):
                n = G * 2 + half
                base = n * 6
                dve.wait_ge(ln_done, n + 1)
                wait(dve, rows_ps, n - 1)
                wait(dve, sub_step, base)
                columns = lambda r: subT[:, half, :, :, r].rearrange("p q j -> p j q")
                nc.vector.tensor_tensor(sub[:, 0], nmax[:, par, :, half * 4:half * 4 + 4], lnd[:, half],
                                        ALU.subtract).then_inc(sub_step, 1)
                for r in range(2):
                    dve.wait_ge(sub_step, base + 2 * r + 1)
                    nc.vector.tensor_copy(columns(r), sub[:, r]).then_inc(sub_step, 1)
                    dve.wait_ge(sub_step, base + 2 * r + 2)
                    nc.vector.tensor_tensor(sub[:, r + 1], sub[:, r], columns(r), ALU.subtract).then_inc(sub_step, 1)
                dve.wait_ge(sub_step, base + 5)
                nc.vector.tensor_copy(columns(2), sub[:, 2]).then_inc(sub_step, 1)

            def take_rows(G, half):
                dve.wait_ge(rows_ps, G * 2 + half + 1)
                wait(dve, rows_loaded[half], G * 64)
                nc.vector.tensor_copy(sub_rows[:, half, :], misc[:]).then_inc(rows_read, 1)

            def take_out(b, hg, half):
                g = b * HG + hg
                dve.wait_ge(tr_ps, g * 2 + half + 1)
                if isinstance(g, int) and g == 0 and half == 0:
                    dve.wait_ge(spiking.gate_stored, NC * 16)
                    dve.wait_ge(spiking.shift_stored, NC * 16)
                if hg == 0:
                    wait(dve, out_stored[half], b * 64)
                nc.vector.tensor_copy(tok[:, half * 4:half * 4 + 4, hg * P:(hg + 1) * P],
                                      misc[:].rearrange("p (q e) -> p q e", q=4)).then_inc(tr_read, 1)

            def finish_statistics(b, half, t):
                F = b * 2 + half
                if t == 0:
                    dve.wait_ge(tr_read, b * 8 + 7 + half)
                wait(dve, fin_stat, (F - 1) * 9 + t + 5)
                nc.vector.bn_stats(fst[:, t, :], tok[:, half * 4 + t, :]).then_inc(fin_stat, 1)
                if t == 3:
                    wait(dve, fin_norm, F * 4)
                    dve.wait_ge(fin_stat, F * 9 + 4)
                    nc.vector.memset(frs[:, 7, :], 0.0)
                    for i in range(4):
                        nc.vector.bn_aggr(fmv[:, i, :], fst[:, i, :]).then_inc(fin_stat, 1)
                    dve.wait_ge(fin_stat, F * 9 + 8)
                    wait(dve, fin_newton, F * 4)
                    nc.vector.tensor_scalar(frs[:, 0, :], fmv[:, :, 1], LN_EPS, None, ALU.add).then_inc(fin_stat, 1)

            def finish_normalise(b, half, pair):
                F = b * 2 + half
                if pair == 0:
                    dve.wait_ge(fin_guess, F + 1)
                    nc.vector.tensor_tensor(frs[:, 3, :], frs[:, 2, :], frs[:, 2, :], ALU.mult).then_inc(fin_newton, 1)
                    dve.wait_ge(fin_newton, F * 4 + 1)
                    nc.vector.tensor_tensor(frs[:, 4, :], frs[:, 3, :], frs[:, 0, :], ALU.mult).then_inc(fin_newton, 1)
                    dve.wait_ge(fin_newton, F * 4 + 2)
                    nc.vector.tensor_scalar(frs[:, 5, :], frs[:, 4, :], -0.5, 1.5, ALU.mult, ALU.add).then_inc(fin_newton, 1)
                    dve.wait_ge(fin_newton, F * 4 + 3)
                    nc.vector.tensor_tensor(frs[:, 6, :], frs[:, 5, :], frs[:, 2, :], ALU.mult).then_inc(fin_newton, 1)
                    dve.wait_ge(fin_newton, F * 4 + 4)
                for t in (2 * pair, 2 * pair + 1):
                    row = tok[:, half * 4 + t, :]
                    nc.vector.tensor_scalar(row, row, fmv[:, t, 0:1], frs[:, 6, t:t + 1],
                                            ALU.subtract, ALU.mult).then_inc(fin_norm, 1)

            def take_misc(b, hg, s, h):
                if h == 4 and s.prev:
                    copy_acc(s.g - 1, 1 - s.par, 1)
                if h == 20 and s.main:
                    copy_acc(s.g, s.par, 0)
                if h - PARTS in V_HALVES and s.scores:
                    take_v(s, V_HALVES.index(h - PARTS))
                if h == 11 and s.main:
                    take_rows(s.g, 1)
                if h == 12 and s.prev:
                    take_out(*before(b, hg), 1)
                if h == 14 and s.scores:
                    take_values(s)
                if h - PARTS in QK_HALVES and s.project:
                    take_qk(s.g, QK_HALVES.index(h - PARTS))
                if h == 23 and s.main:
                    take_out(b, hg, 0)
                if h == 27 and s.scores:
                    take_rows(s.g + 1, 0)

            def slot(b, hg):
                s = Slot(b, hg)
                for h in range(2 * SLOT_STEPS):
                    k, second = h // 2, h % 2
                    tiles = s.tiles(k)
                    take_misc(b, hg, s, h)
                    if isinstance(s.g, int) and s.g < 0 and (s.g, h) in RECURRENCES:
                        for i in RECURRENCES[s.g, h]:
                            spiking.recurrence(NC - 1, i)
                    if tiles:
                        row_max(tiles[0], tiles[1], tiles[2] + second)
                    if s.main and k >= 1 and not second:
                        add_bias(dve, nc.vector, DVE_HEADS, add_dve, b, hg, k - 1)
                    elif s.prev and h == 0:
                        add_bias(dve, nc.vector, DVE_HEADS, add_dve, *before(b, hg), SLOT_STEPS - 1)
                    if h == 7 and s.main:
                        subtracted(s.g, s.par, 1)
                    if h == 23 and s.scores:
                        subtracted(s.g + 1, 1 - s.par, 0)
                    if s.finish0 and 23 <= h < 27:
                        finish_statistics(b, 0, h - 23)
                    if s.finish0 and h in (29, 30):
                        finish_normalise(b, 0, h - 29)
                    if s.finish1 and 12 <= h < 16:
                        finish_statistics(b - 1, 1, h - 12)
                    if s.finish1 and h in (18, 19):
                        finish_normalise(b - 1, 1, h - 18)

            nc.vector.memset(subT[:], 0.0).then_inc(consts, 1)
            nc.vector.memset(before_key[:], 0.0).then_inc(consts, 1)
            nc.vector.tensor_copy(identh[:], w["ident"][:]).then_inc(consts, 1)
            nc.vector.memset(kst[ROWS:ROWS + SUBTRACTED], 1.0).then_inc(consts, 1)
            dve.wait_ge(consts, 4)
            for t in range(TB - 1):
                nc.vector.memset(before_key[:, t, t + 1:], 1.0).then_inc(consts, 1)
            dve.wait_ge(const_loaded, 64)
            spiking.recurrence(NC - 2, 13)
            slots(dve, slot)
            add_bias(dve, nc.vector, DVE_HEADS, add_dve, NB - 1, HG - 1, SLOT_STEPS - 1)
            copy_acc(NG - 1, (NG - 1) % 2, 1)
            take_out(NB - 1, HG - 1, 1)
            for t in range(4):
                finish_statistics(NB - 1, 1, t)
            finish_normalise(NB - 1, 1, 0)
            finish_normalise(NB - 1, 1, 1)

        @block.gpsimd
        def _(pool):
            def finish(b, i, step):
                n = b * TB + i
                row = tok[:, i, :]
                if step == 0:
                    pool.wait_ge(fin_norm, n + 1)
                    pool.wait_ge(fin_loaded[i % 4], (b * 2 + i // 4 + 1) * 32)
                    nc.gpsimd.tensor_tensor(row, row, gain_t[:, i % 4, :], ALU.mult).then_inc(fin_step, 1)
                else:
                    pool.wait_ge(fin_step, n * 2 + 1)
                    nc.gpsimd.tensor_tensor(row, row, shift_t[:, i % 4, :], ALU.add).then_inc(fin_step, 1)

            def slot(b, hg):
                s = Slot(b, hg)
                for k in range(SLOT_STEPS):
                    if s.main and k >= 1:
                        add_bias(pool, nc.gpsimd, POOL_HEADS, add_pool, b, hg, k - 1)
                    elif s.prev and k == 0:
                        add_bias(pool, nc.gpsimd, POOL_HEADS, add_pool, *before(b, hg), SLOT_STEPS - 1)
                    if s.finish0 and k == 15:
                        finish(b, 0, 0)
                    if s.finish1:
                        for n in FINISH_OPS.get(k, ()):
                            finish(b - 1, n // 2, n % 2)

            for c in (NC - 2, NC - 1):
                spiking.fold(c)
            slots(pool, slot)
            add_bias(pool, nc.gpsimd, POOL_HEADS, add_pool, NB - 1, HG - 1, SLOT_STEPS - 1)
            for n in range(1, 2 * TB):
                finish(NB - 1, n // 2, n % 2)


def attention_gated_by_spikes(nc, x, fcT, prT, qT, kT, vT, tableT, gamma, beta, out):
    tokens = x.shape[0]
    xnT = nc.dram_tensor("xnT", [tokens // 512, 2, EB * P, 512], F16).ap()
    gain = nc.dram_tensor("gain", [tokens, EB * P], F32).ap()
    shift = nc.dram_tensor("shift", [tokens, EB * P], F32).ap()
    table_ext = nc.dram_tensor("table_ext", [tableT.shape[0], TABLE_COLS], F32).ap()
    table_rows = nc.dram_tensor("table_rows", [tableT.shape[0], P, TABLE_COLS], F32).ap()
    d = dict(x=x, fcT=fcT, prT=prT, qT=qT, kT=kT, vT=vT, tableT=tableT, gamma=gamma, beta=beta,
             table_ext=table_ext, table_rows=table_rows, xnT=xnT, gain=gain, shift=shift, out=out)
    with ExitStack() as ctx:
        sb = lambda name, shape, dt: ctx.enter_context(nc.sbuf_tensor(name, shape, dt))
        w = {m: sb(f"w_{m}", [P, 2, EB, 512], F16) for m in "qkv"}
        w["unscale"] = sb("unscale", [P, 4], F32)
        w["ident"] = sb("ident", [P, P], F32)
        spiking = SpikingGate(nc, ctx, d)
        with ExitStack() as first:
            w["fc"] = first.enter_context(nc.sbuf_tensor("w_fc", [P, 2, EB, 2048], F16))
            w["pr"] = first.enter_context(nc.sbuf_tensor("w_pr", [P, 2, FB, 512], F16))
            prepare_weights(nc, d, w, spiking)
            feed_forward(nc, d, w, spiking, tokens // 512)
        attention(nc, d, w, spiking, tokens // S)


def kernel(**inputs):
    import numpy as _np
    import concourse.bacc as _bacc
    from concourse import mybir as _mybir
    from concourse.bass_utils import run_bass_kernel_spmd as _run

    laid_out = {
        "in_x": inputs["L0_attn_x"].reshape(-1, 512),
        "in_fcT": inputs["L0_ffn_W_fc"].T,
        "in_prT": inputs["L0_ffn_W_proj"].T,
        "in_qT": inputs["L0_attn_Wq"].T,
        "in_kT": inputs["L0_attn_Wk"].T,
        "in_vT": inputs["L0_attn_Wv"].T,
        "in_tableT": inputs["L0_attn_bias_table"].T,
        "in_gamma": inputs["L0_attn_ln_gamma"],
        "in_beta": inputs["L0_attn_ln_beta"],
    }
    nc = _bacc.Bacc("TRN2", target_bir_lowering=False, num_devices=1)
    arrays, args = {}, []
    for name, a in laid_out.items():
        a = _np.ascontiguousarray(a)
        arrays[name] = a
        args.append(nc.dram_tensor(name, a.shape, _mybir.dt.from_np(a.dtype), kind="ExternalInput").ap())
    tokens, width = laid_out["in_x"].shape
    args.append(nc.dram_tensor("result", (tokens, width), _mybir.dt.float32, kind="ExternalOutput").ap())
    attention_gated_by_spikes(nc, *args)
    r = _run(nc, [arrays], core_ids=[0])
    return r.results[0]["result"].reshape(inputs["L0_attn_x"].shape)
```
